# Optimizing a Trainium2 kernel written in Bass

```python
import numpy as np
import jax
import jax.numpy as jnp

def _softmax(x, axis=-1):
    return jax.nn.softmax(x, axis=axis)

def _gelu(x):
    return jax.nn.gelu(x, approximate=True)

def _silu(x):
    return jax.nn.silu(x)

def _sigmoid(x):
    return jax.nn.sigmoid(x)

def _layernorm(x, axis=-1, eps=1e-05):
    m = jnp.mean(x, axis=axis, keepdims=True)
    v = jnp.var(x, axis=axis, keepdims=True)
    return (x - m) / jnp.sqrt(v + eps)

def _scatter_add(tgt, idx, src, axis=0):
    return tgt.at[idx].add(src)

def _segment_sum(src, seg, n):
    return jax.ops.segment_sum(src, seg, n)
kernel_name = 'mk_macaron_d1_jaxref_r8_1b31dc'

def setup_inputs(seed: int=0):
    np.random.seed(seed)
    _w = jnp.asarray

    def _L0_attn_setup():
        import jax, jax.numpy as jnp
        import numpy as np
        HIDDEN = 128
        NUM_HEADS = 16
        HEAD_DIM = 64
        NUM_KV_HEADS = 4

        def _xavier(key, out_dim, in_dim):
            limit = jnp.sqrt(6.0 / (in_dim + out_dim)).astype(jnp.float32)
            return jax.random.uniform(key, (out_dim, in_dim), jnp.float32, -limit, limit)
        key = jax.random.key(seed)
        kx, kq, kk, kv, ko = jax.random.split(key, 5)
        return {'hidden_states': jax.random.normal(kx, (2, 256, HIDDEN), jnp.float32), 'Wq': _xavier(kq, NUM_HEADS * HEAD_DIM, HIDDEN), 'Wk': _xavier(kk, NUM_KV_HEADS * HEAD_DIM, HIDDEN), 'Wv': _xavier(kv, NUM_KV_HEADS * HEAD_DIM, HIDDEN), 'Wo': _xavier(ko, HIDDEN, NUM_HEADS * HEAD_DIM)}
    _L0_attn_in = _L0_attn_setup()

    def _L0_ffn_setup():
        import jax, jax.numpy as jnp
        import numpy as np
        D_MODEL = 128
        D_FF = 512
        N_EXPERTS = 8
        TOP_K = 2
        BATCH, SEQ = (4, 128)
        key = jax.random.key(seed)
        ks = jax.random.split(key, 5)
        x = jax.random.normal(ks[0], (BATCH, SEQ, D_MODEL), jnp.float32)
        Wr = jax.random.normal(ks[1], (D_MODEL, N_EXPERTS), jnp.float32) * D_MODEL ** (-0.5)
        W1 = jax.random.normal(ks[2], (N_EXPERTS, D_MODEL, D_FF), jnp.float32) * D_MODEL ** (-0.5)
        b1 = jnp.zeros((N_EXPERTS, D_FF), jnp.float32)
        W2 = jax.random.normal(ks[3], (N_EXPERTS, D_FF, D_MODEL), jnp.float32) * D_FF ** (-0.5)
        b2 = jnp.zeros((N_EXPERTS, D_MODEL), jnp.float32)
        return {'x': x, 'Wr': Wr, 'W1': W1, 'b1': b1, 'W2': W2, 'b2': b2}
    _L0_ffn_in = _L0_ffn_setup()
    _d = {'L0_attn_hidden_states': _L0_attn_in['hidden_states'], 'L0_attn_Wq': _L0_attn_in['Wq'], 'L0_attn_Wk': _L0_attn_in['Wk'], 'L0_attn_Wv': _L0_attn_in['Wv'], 'L0_attn_Wo': _L0_attn_in['Wo'], 'L0_ffn_Wr': _L0_ffn_in['Wr'], 'L0_ffn_W1': _L0_ffn_in['W1'], 'L0_ffn_b1': _L0_ffn_in['b1'], 'L0_ffn_W2': _L0_ffn_in['W2'], 'L0_ffn_b2': _L0_ffn_in['b2']}
    _x0 = _d['L0_attn_hidden_states']
    _d['L0_attn_hidden_states'] = jax.random.normal(jax.random.fold_in(jax.random.key(seed), 1), (4, 1024, 128), dtype=_x0.dtype)
    del _x0
    return _d

def reference(L0_attn_hidden_states, L0_attn_Wq, L0_attn_Wk, L0_attn_Wv, L0_attn_Wo, L0_ffn_Wr, L0_ffn_W1, L0_ffn_b1, L0_ffn_W2, L0_ffn_b2):

    def _L0_attn_ref(hidden_states, Wq, Wk, Wv, Wo):
        import jax, jax.numpy as jnp
        import numpy as np
        HIDDEN = 128
        NUM_HEADS = 16
        HEAD_DIM = 64
        NUM_KV_HEADS = 4

        def _xavier(key, out_dim, in_dim):
            limit = jnp.sqrt(6.0 / (in_dim + out_dim)).astype(jnp.float32)
            return jax.random.uniform(key, (out_dim, in_dim), jnp.float32, -limit, limit)
        B, S, _ = hidden_states.shape
        q = (hidden_states @ Wq.T).reshape(B, S, NUM_HEADS, HEAD_DIM).transpose(0, 2, 1, 3)
        k = (hidden_states @ Wk.T).reshape(B, S, NUM_KV_HEADS, HEAD_DIM).transpose(0, 2, 1, 3)
        v = (hidden_states @ Wv.T).reshape(B, S, NUM_KV_HEADS, HEAD_DIM).transpose(0, 2, 1, 3)
        n_rep = NUM_HEADS // NUM_KV_HEADS
        if n_rep > 1:
            k = jnp.repeat(k, n_rep, axis=1)
            v = jnp.repeat(v, n_rep, axis=1)
        scale = HEAD_DIM ** (-0.5)
        scores = jnp.einsum('bhqd,bhkd->bhqk', q, k) * scale
        causal = jnp.triu(jnp.full((S, S), -jnp.inf, dtype=scores.dtype), k=1)
        scores = scores + causal[None, None]
        probs = jax.nn.softmax(scores, axis=-1)
        out = jnp.einsum('bhqk,bhkd->bhqd', probs, v)
        out = out.transpose(0, 2, 1, 3).reshape(B, S, NUM_HEADS * HEAD_DIM)
        return out @ Wo.T

    def _L0_ffn_ref(x, Wr, W1, b1, W2, b2):
        import jax, jax.numpy as jnp
        import numpy as np
        D_MODEL = 128
        D_FF = 512
        N_EXPERTS = 8
        TOP_K = 2
        BATCH, SEQ = (4, 128)
        B, S, D = x.shape
        E = Wr.shape[1]
        xf = x.reshape(-1, D)
        probs = jax.nn.softmax(xf @ Wr, axis=-1)
        top_v, top_i = jax.lax.top_k(probs, TOP_K)
        gates = top_v / jnp.sum(top_v, axis=-1, keepdims=True)
        cw = jnp.sum(gates[:, :, None] * jax.nn.one_hot(top_i, E, dtype=x.dtype), axis=1)
        out = jnp.zeros_like(xf)
        for e in range(E):
            h = jax.nn.relu(xf @ W1[e] + b1[e])
            y = h @ W2[e] + b2[e]
            out = out + cw[:, e:e + 1] * y
        return out.reshape(x.shape)
    x = L0_attn_hidden_states
    x = x + 0.5 * _L0_ffn_ref(_layernorm(x, axis=-1), L0_ffn_Wr, L0_ffn_W1, L0_ffn_b1, L0_ffn_W2, L0_ffn_b2)
    x = x + _L0_attn_ref(_layernorm(x, axis=-1), L0_attn_Wq, L0_attn_Wk, L0_attn_Wv, L0_attn_Wo)
    x = x + 0.5 * _L0_ffn_ref(_layernorm(x, axis=-1), L0_ffn_Wr, L0_ffn_W1, L0_ffn_b1, L0_ffn_W2, L0_ffn_b2)
    return x

_drawn_inputs = setup_inputs


def setup_inputs(seed=0):
    import zlib

    import numpy as np

    out = dict(_drawn_inputs(seed))
    spreads = {'L0_ffn_b1': (0.0, 0.1), 'L0_ffn_b2': (0.0, 0.1)}
    factors = {}
    for name, (base, spread) in spreads.items():
        noise = np.random.default_rng([zlib.crc32(name.encode()), seed]).standard_normal(out[name].shape)
        drawn = base * np.exp(spread * noise) if base else spread * noise
        out[name] = jnp.asarray(drawn.astype(out[name].dtype))
    for name, factor in factors.items():
        out[name] = (out[name] * factor).astype(out[name].dtype)
    return out
```

```python
from contextlib import ExitStack

import concourse.bass as bass
from concourse import mybir

ALU = mybir.AluOpType
ACT = mybir.ActivationFunctionType
AX = mybir.AxisListType
F32 = mybir.dt.float32
F32R = mybir.dt.float32r
BF16 = mybir.dt.bfloat16

P = 128
BATCH, SEQ = 4, 1024
TOKENS = BATCH * SEQ
CHUNK = 512
TPC = CHUNK // P
CHUNKS = TOKENS // CHUNK
EXPERTS, FF, TOP_K = 8, 512, 2
FSL = FF // P
HEADS, KV_HEADS, HEAD = 16, 4, 64
QPK = HEADS // KV_HEADS
EPS = 1e-5
STRUCK = -1e30
IDLE = SEQ // P


class Chain:

    def __init__(self, engine, sem, base):
        self.engine, self.sem, self.base, self.n = engine, sem, base, 0

    def link(self, instruction):
        self.n += 1
        instruction.then_inc(self.sem, 1)
        self.engine.wait_ge(self.sem, self.base + self.n)


def ffn_phase(nc, tag, x_rows, w1_in, w2_in, b1_in, b2_in, wr_in, load_x=None, store_x=None):
    with ExitStack() as ctx:
        def sb(name, shape, dt=F32):
            return ctx.enter_context(nc.sbuf_tensor(f"{name}_{tag}", shape, dt))

        def psum(name):
            return ctx.enter_context(nc.psum_tensor(f"{name}_{tag}", [P, CHUNK], F32))

        def sem(name):
            return ctx.enter_context(nc.semaphore(f"{name}_{tag}"))

        w1_raw = sb("w1_raw", [P, EXPERTS, FF])
        w2_raw = sb("w2_raw", [P, EXPERTS, FF])
        w1_hi = sb("w1_hi", [P, EXPERTS, FF], F32R)
        w1_lo = sb("w1_lo", [P, EXPERTS, FF], F32R)
        w2_hi = sb("w2_hi", [P, EXPERTS, FF], F32R)
        w2_lo = sb("w2_lo", [P, EXPERTS, FF], F32R)
        b1 = sb("b1", [P, EXPERTS * FSL])
        b2 = sb("b2", [P, EXPERTS])
        wr_raw = sb("wr_raw", [P, EXPERTS])
        wr_parts = sb("wr_parts", [P, 2 * EXPERTS], F32R)
        ident = sb("ident", [P, P])
        spread = sb("spread", [2 * EXPERTS, EXPERTS, P])
        spread_r = sb("spread_r", [2 * EXPERTS, EXPERTS, P], F32R)
        earlier = sb("earlier", [P, EXPERTS, EXPERTS])
        minus_half = sb("minus_half", [P, TPC])
        row_sum = sb("row_sum", [P, TPC])
        mean = sb("mean", [P, TPC])
        centred = sb("centred", [P, TPC, P])
        squares = sb("squares", [P, TPC, P])
        sq_sum = sb("sq_sum", [P, TPC])
        var_eps = sb("var_eps", [P, TPC])
        rstd = sb("rstd", [P, TPC])
        xn = sb("xn", [P, TPC, P])
        xT_hi = sb("xT_hi", [P, 2, CHUNK], F32R)
        xT_lo = sb("xT_lo", [P, 2, CHUNK], F32R)
        part = sb("part", [P, TPC, 2 * EXPERTS])
        logits = sb("logits", [P, TPC, EXPERTS])
        top = sb("top", [P, TPC])
        shifted = sb("shifted", [P, TPC, EXPERTS])
        weight = sb("weight", [P, TPC, EXPERTS])
        above = sb("above", [P, TPC, EXPERTS, EXPERTS])
        equal = sb("equal", [P, TPC, EXPERTS, EXPERTS])
        rank = sb("rank", [P, TPC, EXPERTS])
        chosen = sb("chosen", [P, TPC, EXPERTS])
        picked = sb("picked", [P, TPC, EXPERTS])
        pair_sum = sb("pair_sum", [P, TPC])
        twice_sum = sb("twice_sum", [P, TPC])
        inverse = sb("inverse", [P, TPC])
        gate = sb("gate", [P, TPC, EXPERTS])
        gate_hi = sb("gate_hi", [P, TPC, EXPERTS], F32R)
        gate_parts = sb("gate_parts", [P, TPC, 2 * EXPERTS])
        gateT = sb("gateT", [2 * EXPERTS, 2, CHUNK], F32R)
        h = sb("h", [P, 4, CHUNK])
        h_hi = sb("h_hi", [P, 4, CHUNK], F32R)
        h_lo = sb("h_lo", [P, 4, CHUNK], F32R)
        gate_all = sb("gate_all", [P, 2, CHUNK])
        gated = sb("gated", [P, 2, CHUNK])
        acc = sb("acc", [P, CHUNK])

        ps_x = psum("ps_x")
        ps_r = psum("ps_r")
        ps_g = psum("ps_g")
        ps_h = [psum("ps_h0"), psum("ps_h1")]
        ps_y = [psum("ps_y0"), psum("ps_y1")]
        ps_o = psum("ps_o")

        rows_in = sem("rows_in")
        small_in = sem("small_in")
        w_in = [sem(f"w_in{i}") for i in range(EXPERTS)]
        consts = sem("consts")
        w_upper = sem("w_upper")
        w_lower = sem("w_lower")
        prep = sem("prep")
        var_ready = sem("var_ready")
        rstd_ready = sem("rstd_ready")
        xn_ready = sem("xn_ready")
        xT_done = sem("xT_done")
        xhi_ready = sem("xhi_ready")
        xlo_ready = sem("xlo_ready")
        logits_done = sem("logits_done")
        shift_ready = sem("shift_ready")
        exp_ready = sem("exp_ready")
        gate_ready = sem("gate_ready")
        gateT_done = sem("gateT_done")
        gateT_ready = sem("gateT_ready")
        spread_done = sem("spread_done")
        spread_ready = sem("spread_ready")
        h_done = sem("h_done")
        relu_done = sem("relu_done")
        hhi_ready = sem("hhi_ready")
        hlo_ready = sem("hlo_ready")
        h_used = sem("h_used")
        gated_ready = sem("gated_ready")
        acc_done = sem("acc_done")
        outT_done = sem("outT_done")
        x_updated = sem("x_updated")
        stored = sem("stored")

        HSTEPS = EXPERTS * FSL
        LAG = 3
        ADDS = EXPERTS - 1
        PREP = 21

        block = ctx.enter_context(nc.Block())

        @block.sync
        def _(sp):
            if load_x is not None:
                load_x(sp, rows_in)
            sp.dma_start(wr_raw[:], wr_in).then_inc(small_in, 16)
            sp.dma_start(b1[:], b1_in).then_inc(small_in, 16)
            sp.dma_start(b2[:], b2_in).then_inc(small_in, 16)
            for e in range(EXPERTS):
                sp.dma_start(w1_raw[:, e, :], w1_in[e]).then_inc(w_in[e], 16)
                sp.dma_start(w2_raw[:, e, :].rearrange("p (f d) -> p f d", f=FSL),
                             w2_in[e].rearrange("(f p) d -> p f d", p=P)).then_inc(w_in[e], 16)
            if store_x is not None:
                with sp.Fori(0, CHUNKS) as c:
                    sp.wait_ge(x_updated, c + 2)
                    store_x(sp, c, stored)
                sp.wait_ge(stored, 16 * CHUNKS)

        @block.gpsimd
        def _(pool):
            nc.gpsimd.memset(ident[:], 0.0).then_inc(consts, 1)
            nc.gpsimd.memset(spread[:], 0.0).then_inc(consts, 1)
            nc.gpsimd.memset(earlier[:], 0.0).then_inc(consts, 1)
            nc.gpsimd.memset(minus_half[:], -0.5).then_inc(consts, 1)
            pool.wait_ge(consts, 4)
            nc.gpsimd.affine_select(out=ident[:], in_=ident[:], compare_op=ALU.not_equal, fill=1.0, base=0,
                                    pattern=[[-1, P]], channel_multiplier=1).then_inc(consts, 1)
            nc.gpsimd.affine_select(out=spread[:], in_=spread[:], compare_op=ALU.not_equal, fill=1.0, base=0,
                                    pattern=[[-1, EXPERTS], [0, P]], channel_multiplier=1).then_inc(consts, 1)
            nc.gpsimd.affine_select(out=earlier[:], in_=earlier[:], compare_op=ALU.is_ge, fill=1.0, base=0,
                                    pattern=[[-1, EXPERTS], [1, EXPERTS]], channel_multiplier=0).then_inc(consts, 1)
            pool.wait_ge(consts, 7)
            nc.gpsimd.affine_select(out=spread[:], in_=spread[:], compare_op=ALU.not_equal, fill=1.0,
                                    base=-EXPERTS, pattern=[[-1, EXPERTS], [0, P]],
                                    channel_multiplier=1).then_inc(consts, 1)
            nc.gpsimd.memset(acc[:], 0.0).then_inc(acc_done, 1)

            def rstd_of(k):
                pool.wait_ge(var_ready, k + 1)
                nc.gpsimd.tensor_tensor(rstd[:], var_eps[:], minus_half[:], ALU.pow).then_inc(rstd_ready, 1)

            rstd_of(0)
            with pool.Fori(0, CHUNKS) as c:
                rstd_of(c + 1)
                for e in range(1, EXPERTS):
                    pool.wait_ge(gated_ready, EXPERTS * c + (e + 1))
                    if e == 1:
                        pool.wait_ge(outT_done, c + 1)
                        first = gated[:, 0, :]
                    else:
                        pool.wait_ge(acc_done, ADDS * c + e)
                        first = acc[:]
                    nc.gpsimd.tensor_tensor(acc[:], first, gated[:, e % 2, :], ALU.add).then_inc(acc_done, 1)

        @block.scalar
        def _(act):
            def transpose_hi(k, slot):
                act.wait_ge(xT_done, k + 1)
                nc.scalar.activation(xT_hi[:, slot, :], ps_x[:], ACT.Copy).then_inc(xhi_ready, 1)

            def exp_of(k):
                act.wait_ge(shift_ready, k + 1)
                nc.scalar.activation(weight[:], shifted[:], ACT.Exp).then_inc(exp_ready, 1)

            def gateT_of(k, slot):
                act.wait_ge(gateT_done, k + 1)
                nc.scalar.activation(gateT[:, slot, :], ps_r[0:2 * EXPERTS, :], ACT.Copy).then_inc(gateT_ready, 1)

            act.wait_ge(small_in, 48)
            nc.scalar.activation(wr_parts[:, 0:EXPERTS], wr_raw[:], ACT.Copy).then_inc(w_upper, 1)
            act.wait_ge(consts, 8)
            nc.scalar.activation(spread_r[:], spread[:], ACT.Copy).then_inc(w_upper, 1)
            transpose_hi(0, 0)
            exp_of(0)
            for e in range(EXPERTS):
                act.wait_ge(w_in[e], 32)
                nc.scalar.activation(w1_hi[:, e, :], w1_raw[:, e, :], ACT.Copy)
                nc.scalar.activation(w2_hi[:, e, :], w2_raw[:, e, :], ACT.Copy).then_inc(w_upper, 1)
                if e == 0:
                    gateT_of(0, 0)
            with act.Fori(0, CHUNKS // 2) as pair:
                for half in range(2):
                    c = 2 * pair + half
                    for n in range(HSTEPS):
                        e, f = divmod(n, FSL)
                        if f == 0:
                            act.wait_ge(spread_done, EXPERTS * c + (e + 1))
                            if e >= 2:
                                act.wait_ge(gated_ready, EXPERTS * c + (e - 1))
                            nc.scalar.activation(gate_all[:, e % 2, :], ps_g[:], ACT.Copy).then_inc(spread_ready, 1)
                        act.wait_ge(h_done, HSTEPS * c + (n + 1))
                        if n >= 4:
                            act.wait_ge(hlo_ready, HSTEPS * c + (n - 3))
                        nc.scalar.activation(h[:, n % 4, :], ps_h[n % 2][:], ACT.Relu,
                                             bias=b1[:, n:n + 1]).then_inc(relu_done, 1)
                        if n == 9:
                            transpose_hi(c + 1, 1 - half)
                        if n == 18:
                            exp_of(c + 1)
                        if n == 26:
                            gateT_of(c + 1, 1 - half)

        @block.vector
        def _(dve):
            def rows_at(slot):
                if isinstance(slot, int):
                    return x_rows[:, slot * TPC:(slot + 1) * TPC, :]
                return x_rows[:, bass.ds(slot * TPC, TPC), :]

            def over(stat, width):
                return stat[:].unsqueeze(2).to_broadcast([P, TPC, width])


            def prepare(k, slot):
                chain = Chain(dve, prep, PREP * k)

                def norm():
                    chain.link(nc.vector.tensor_reduce(row_sum[:], rows_at(k + 1), AX.X, ALU.add))
                    chain.link(nc.vector.tensor_scalar(mean[:], row_sum[:], 1.0 / P, None, ALU.mult))
                    chain.link(nc.vector.tensor_tensor(centred[:], rows_at(k + 1), over(mean, P), ALU.subtract))
                    chain.link(nc.vector.tensor_tensor(squares[:], centred[:], centred[:], ALU.mult))
                    chain.link(nc.vector.tensor_reduce(sq_sum[:], squares[:], AX.X, ALU.add))
                    nc.vector.tensor_scalar(var_eps[:], sq_sum[:], 1.0 / P, EPS, ALU.mult, ALU.add).then_inc(var_ready, 1)

                def scale():
                    dve.wait_ge(rstd_ready, k + 1)
                    nc.vector.tensor_tensor(xn[:], centred[:], over(rstd, P), ALU.mult).then_inc(xn_ready, 1)

                def lower():
                    dve.wait_ge(xhi_ready, k + 1)
                    nc.vector.tensor_tensor(xT_lo[:, slot, :], ps_x[:], xT_hi[:, slot, :].bitcast(F32),
                                            ALU.subtract).then_inc(xlo_ready, 1)

                def route():
                    dve.wait_ge(logits_done, k + 1)
                    chain.link(nc.vector.tensor_copy(
                        part[:], ps_r[:, 0:TPC * 2 * EXPERTS].rearrange("p (t e) -> p t e", t=TPC)))
                    chain.link(nc.vector.tensor_tensor(logits[:], part[:, :, 0:EXPERTS], part[:, :, EXPERTS:],
                                                       ALU.add))
                    chain.link(nc.vector.tensor_reduce(top[:], logits[:], AX.X, ALU.max))
                    nc.vector.tensor_tensor(shifted[:], logits[:], over(top, EXPERTS),
                                            ALU.subtract).then_inc(shift_ready, 1)

                def rank_experts():
                    square = [P, TPC, EXPERTS, EXPERTS]
                    one = logits[:].unsqueeze(3).to_broadcast(square)
                    other = logits[:].unsqueeze(2).to_broadcast(square)
                    before = earlier[:].unsqueeze(1).to_broadcast(square)
                    chain.link(nc.vector.tensor_tensor(equal[:], other, one, ALU.is_equal))
                    chain.link(nc.vector.tensor_tensor(above[:], other, one, ALU.is_gt))
                    chain.link(nc.vector.tensor_tensor(equal[:], equal[:], before, ALU.mult))
                    chain.link(nc.vector.tensor_tensor(above[:], above[:], equal[:], ALU.add))
                    chain.link(nc.vector.tensor_reduce(rank[:], above[:], AX.X, ALU.add))
                    chain.link(nc.vector.tensor_scalar(chosen[:], rank[:], float(TOP_K), None, ALU.is_lt))

                def gates():
                    dve.wait_ge(exp_ready, k + 1)
                    chain.link(nc.vector.tensor_tensor(picked[:], weight[:], chosen[:], ALU.mult))
                    chain.link(nc.vector.tensor_reduce(pair_sum[:], picked[:], AX.X, ALU.add))
                    chain.link(nc.vector.tensor_scalar(twice_sum[:], pair_sum[:], 2.0, None, ALU.mult))
                    chain.link(nc.vector.reciprocal(inverse[:], twice_sum[:]))
                    chain.link(nc.vector.tensor_tensor(gate[:], picked[:], over(inverse, EXPERTS), ALU.mult))
                    chain.link(nc.vector.tensor_copy(gate_hi[:], gate[:]))
                    chain.link(nc.vector.tensor_copy(gate_parts[:, :, 0:EXPERTS], gate_hi[:].bitcast(F32)))
                    nc.vector.tensor_tensor(gate_parts[:, :, EXPERTS:], gate[:], gate_hi[:].bitcast(F32),
                                            ALU.subtract).then_inc(gate_ready, 1)
                    assert chain.n == PREP, chain.n

                return norm, scale, lower, route, rank_experts, gates

            def gate_y(c, e):
                dve.wait_ge(h_used, HSTEPS * c + FSL * (e + 1))
                dve.wait_ge(spread_ready, EXPERTS * c + (e + 1))
                if e >= 2:
                    dve.wait_ge(acc_done, ADDS * c + (1 + max(e - 2, 1)))
                nc.vector.scalar_tensor_tensor(out=gated[:, e % 2, :], in0=ps_y[e % 2][:], scalar=b2[:, e:e + 1],
                                               in1=gate_all[:, e % 2, :], op0=ALU.add,
                                               op1=ALU.mult).then_inc(gated_ready, 1)

            def add_rows(slot):
                rows = rows_at(slot)
                nc.vector.tensor_tensor(rows, rows, ps_o[:].rearrange("p (t d) -> p t d", t=TPC),
                                        ALU.add).then_inc(x_updated, 1)

            nc.vector.memset(x_rows[:, 0:TPC, :], 0.0)
            nc.vector.memset(x_rows[:, (CHUNKS + 1) * TPC:, :], 0.0)
            if load_x is not None:
                dve.wait_ge(rows_in, 16 * CHUNKS)
            norm, scale, lower, route, rank_experts, gates = prepare(0, 0)
            norm()
            dve.wait_ge(w_upper, 1)
            nc.vector.tensor_tensor(wr_parts[:, EXPERTS:], wr_raw[:], wr_parts[:, 0:EXPERTS].bitcast(F32),
                                    ALU.subtract).then_inc(w_lower, 1)
            scale()
            lower()
            route()
            dve.wait_ge(consts, 8)
            rank_experts()
            gates()
            for e in range(EXPERTS):
                dve.wait_ge(w_upper, e + 3)
                nc.vector.tensor_tensor(w1_lo[:, e, :], w1_raw[:, e, :], w1_hi[:, e, :].bitcast(F32), ALU.subtract)
                nc.vector.tensor_tensor(w2_lo[:, e, :], w2_raw[:, e, :], w2_hi[:, e, :].bitcast(F32),
                                        ALU.subtract).then_inc(w_lower, 1)

            with dve.Fori(0, CHUNKS // 2) as pair:
                for half in range(2):
                    c = 2 * pair + half
                    norm, scale, lower, route, rank_experts, gates = prepare(c + 1, 1 - half)
                    for n in range(HSTEPS + 1):
                        if n < HSTEPS:
                            dve.wait_ge(relu_done, HSTEPS * c + (n + 1))
                            if n >= 4:
                                dve.wait_ge(h_used, HSTEPS * c + (n - 3))
                            nc.vector.tensor_copy(h_hi[:, n % 4, :], h[:, n % 4, :]).then_inc(hhi_ready, 1)
                        if n >= 1:
                            m = n - 1
                            dve.wait_ge(hhi_ready, HSTEPS * c + (m + 1))
                            nc.vector.tensor_tensor(h_lo[:, m % 4, :], h[:, m % 4, :], h_hi[:, m % 4, :].bitcast(F32),
                                                    ALU.subtract).then_inc(hlo_ready, 1)
                        if n == 2:
                            norm()
                        if n == 5:
                            dve.wait_ge(outT_done, c + 1)
                            add_rows(c)
                        if n == 6:
                            scale()
                        if n == 11:
                            lower()
                        if n == 16:
                            route()
                        if n == 17:
                            rank_experts()
                        if n == 20:
                            gates()
                        if n >= 7 and n % FSL == 3:
                            gate_y(c, (n - 7) // FSL)
                    gate_y(c, EXPERTS - 1)
            dve.wait_ge(outT_done, CHUNKS + 1)
            add_rows(CHUNKS)

        @block.tensor
        def _(pe):
            def transpose_rows(k):
                pe.wait_ge(xn_ready, k + 1)
                for t in range(TPC):
                    last = nc.tensor.transpose(ps_x[:, t * P:(t + 1) * P], xn[:, t, :], ident[:])
                last.then_inc(xT_done, 1)

            def logits_of(k, slot):
                pe.wait_ge(xlo_ready, k + 1)
                for t in range(TPC):
                    out = ps_r[:, t * 2 * EXPERTS:(t + 1) * 2 * EXPERTS]
                    cols = slice(t * P, (t + 1) * P)
                    nc.tensor.matmul(out, xT_hi[:, slot, cols], wr_parts[:], start=True, stop=False)
                    last = nc.tensor.matmul(out, xT_lo[:, slot, cols], wr_parts[:], start=False, stop=True)
                last.then_inc(logits_done, 1)

            def transpose_gates(k):
                pe.wait_ge(gate_ready, k + 1)
                for t in range(TPC):
                    last = nc.tensor.transpose(ps_r[0:2 * EXPERTS, t * P:(t + 1) * P], gate_parts[:, t, :], ident[:])
                last.then_inc(gateT_done, 1)

            def transpose_sum(done):
                pe.wait_ge(acc_done, done)
                for t in range(TPC):
                    last = nc.tensor.transpose(ps_o[:, t * P:(t + 1) * P], acc[:, t * P:(t + 1) * P], ident[:])
                last.then_inc(outT_done, 1)

            pe.wait_ge(consts, 8)
            transpose_rows(0)
            pe.wait_ge(w_lower, 1)
            logits_of(0, 0)
            transpose_gates(0)
            pe.wait_ge(w_lower, 2)
            with pe.Fori(0, CHUNKS // 2) as pair:
                for half in range(2):
                    c = 2 * pair + half
                    for n in range(HSTEPS + LAG):
                        if n < HSTEPS:
                            e, f = divmod(n, FSL)
                            if f == 0:
                                if e == 0:
                                    pe.wait_ge(gateT_ready, c + 1)
                                else:
                                    pe.wait_ge(spread_ready, EXPERTS * c + e)
                                    pe.wait_ge(w_lower, e + 2)
                                nc.tensor.matmul(ps_g[:], spread_r[:, e, :], gateT[:, half, :], start=True,
                                                 stop=True).then_inc(spread_done, 1)
                            if n >= 2:
                                pe.wait_ge(relu_done, HSTEPS * c + (n - 1))
                            fs = slice(f * P, (f + 1) * P)
                            nc.tensor.matmul(ps_h[n % 2][:], w1_hi[:, e, fs], xT_hi[:, half, :], start=True, stop=False)
                            nc.tensor.matmul(ps_h[n % 2][:], w1_hi[:, e, fs], xT_lo[:, half, :], start=False, stop=False)
                            nc.tensor.matmul(ps_h[n % 2][:], w1_lo[:, e, fs], xT_hi[:, half, :], start=False,
                                             stop=True).then_inc(h_done, 1)
                        if n == 4:
                            transpose_sum(ADDS * c + 1)
                        if n == 8:
                            transpose_rows(c + 1)
                        if n == 14:
                            logits_of(c + 1, 1 - half)
                        if n == 24:
                            transpose_gates(c + 1)
                        if n >= LAG:
                            m = n - LAG
                            e, f = divmod(m, FSL)
                            fs = slice(f * P, (f + 1) * P)
                            if f == 0 and e >= 2:
                                pe.wait_ge(gated_ready, EXPERTS * c + (e - 1))
                            pe.wait_ge(hlo_ready, HSTEPS * c + (m + 1))
                            y = ps_y[e % 2][:]
                            nc.tensor.matmul(y, w2_hi[:, e, fs], h_hi[:, m % 4, :], start=(f == 0), stop=False)
                            nc.tensor.matmul(y, w2_hi[:, e, fs], h_lo[:, m % 4, :], start=False, stop=False)
                            last = nc.tensor.matmul(y, w2_lo[:, e, fs], h_hi[:, m % 4, :], start=False,
                                                    stop=(f == FSL - 1))
                            last.then_inc(h_used, 1)
            transpose_sum(ADDS * CHUNKS + 1)


class Item:

    def __init__(self, kind, slot, before, head=0, tile=0):
        self.kind, self.slot, self.head, self.tile = kind, slot, head, tile
        self.done = before[0] + 1
        self.hi = before[1] + (kind in ("xT", "K", "Q"))
        self.act = before[2] + (kind in ("V", "maxT", "y"))
        self.dve = before[3] + (kind in ("xT", "K", "Q", "peak", "out"))
        self.last_is_act = self.act > before[2]


def plan_items(groups):
    count, total, placed = (0, 0, 0, 0), 0, {}
    flat = []
    for place, kinds in groups:
        for kind, head, tile in kinds:
            item = Item(kind, total % 2, count, head, tile)
            count = (item.done, item.hi, item.act, item.dve)
            total += 1
            item.two_before = flat[-2] if len(flat) >= 2 else None
            flat.append(item)
            placed.setdefault(place, []).append(item)
    return placed, count


def attention_phase(nc, x_rows, wq_in, wk_in, wv_in, wo_in):
    with ExitStack() as ctx:
        def sb(name, shape, dt=F32):
            return ctx.enter_context(nc.sbuf_tensor(name, shape, dt))

        def psum(name, width=CHUNK):
            return ctx.enter_context(nc.psum_tensor(name, [P, width], F32))

        def sem(name):
            return ctx.enter_context(nc.semaphore(name))

        SCALE = float(HEAD) ** -0.5
        ST = SEQ // P
        QC = SEQ // CHUNK
        PAIRS = HEADS // 2

        wq_raw = sb("wq_raw", [P, HEADS * HEAD])
        wq_hi = sb("wq_hi", [P, HEADS * HEAD], F32R)
        wq_lo = sb("wq_lo", [P, HEADS * HEAD], F32R)
        wk_raw = sb("wk_raw", [P, KV_HEADS, 2, HEAD])
        wk_hi = sb("wk_hi", [P, KV_HEADS, 2, HEAD], F32R)
        wk_lo = sb("wk_lo", [P, KV_HEADS, 2, HEAD], F32R)
        wv_raw = sb("wv_raw", [P, KV_HEADS * HEAD])
        wv_hi = sb("wv_hi", [P, KV_HEADS * HEAD], F32R)
        wv_lo = sb("wv_lo", [P, KV_HEADS * HEAD], F32R)
        wo = sb("wo", [P, PAIRS, P])
        ident = sb("ident_a", [P, P])
        ident_b = sb("ident_b", [P, P], BF16)
        mask_q = sb("mask_q", [P, P], BF16)
        mask_k = sb("mask_k", [P, P], BF16)
        minus_half = sb("minus_half_a", [P, ST])
        row_sum = sb("row_sum_a", [P, ST])
        mean = sb("mean_a", [P, ST])
        sq_sum = sb("sq_sum_a", [P, ST])
        var_eps = sb("var_eps_a", [P, ST])
        rstd = sb("rstd_a", [P, ST])
        centred = sb("centred_a", [P, ST, P])
        squares = sb("squares_a", [P, ST, P])
        xT_hi = sb("xT_hi_a", [P, SEQ], F32R)
        xT_lo = sb("xT_lo_a", [P, SEQ], F32R)
        q_both = [sb(f"q_both{i}", [P, QPK, SEQ], F32R) for i in range(2)]
        q_max = [sb(f"q_max{i}", [P, QPK, SEQ], F32R) for i in range(2)]
        k_twice = [sb(f"k_twice{i}", [P, SEQ], F32R) for i in range(2)]
        k_low = [sb(f"k_low{i}", [P, SEQ], F32R) for i in range(2)]
        v_ones = [sb(f"v_ones{i}", [P, ST, 2 * HEAD]) for i in range(2)]
        neg_max = sb("neg_max", [P, 2, QPK * ST])
        max_rows = sb("max_rows", [QPK * ST, 2, P], F32R)
        probs = sb("probs", [P, 4, CHUNK])
        inverse = sb("inverse_a", [HEAD, 2, CHUNK])
        oT = sb("oT", [P, PAIRS, SEQ])
        yT = sb("yT", [P, SEQ])

        ps_s = [psum("ps_s0"), psum("ps_s1")]
        ps_v = [psum("ps_v0"), psum("ps_v1")]
        ps_i = [psum("ps_i0", 2 * CHUNK), psum("ps_i1", 2 * CHUNK)]

        w_in = sem("w_in_a")
        consts = sem("consts_a")
        w_upper = sem("w_upper_a")
        w_lower = sem("w_lower_a")
        prep = sem("prep_a")
        var_ready = sem("var_ready_a")
        rstd_ready = sem("rstd_ready_a")
        xn_ready = sem("xn_ready_a")
        item_done = sem("item_done")
        hi_ready = sem("hi_ready")
        act_read = sem("act_read")
        dve_read = sem("dve_read")
        max_in = sem("max_in")
        s_done = sem("s_done")
        exp_done = sem("exp_done")
        pv_done = sem("pv_done")
        inv_done = sem("inv_done")
        head_done = sem("head_done")

        STEPS = [(j, qc, kt) for j in range(QPK) for qc in range(QC) for kt in range((qc + 1) * TPC)]
        NS = len(STEPS)
        LAG = 2
        CHUNKS_U = QPK * QC

        def cols_of(qc, kt):
            first = max(qc * CHUNK, kt * P)
            return first, first - qc * CHUNK

        peaks = [("peak", j, t) for j in range(QPK) for t in range(ST)]

        def unit_groups(g, first):
            late = 3 if first else 0
            groups = [((g, 0), [("xT", 0, 0)])] if first else []
            groups += [((g, late + 1), [("K", 0, 0)]), ((g, late + 2), [("V", 0, 0)]),
                       ((g, late + 3), [("Q", 0, 0)]), ((g, late + 5), [("Q", 2, 0)])]
            groups += [((g, late + 7 + n), [x]) for n, x in enumerate(peaks)]
            groups += [((g, late + 7 + len(peaks) + 3), [("maxT", 0, 0)])]
            return groups

        BODY, PER = plan_items([x for g in range(KV_HEADS) for x in unit_groups(g, g == KV_HEADS - 1)]
                               + [((KV_HEADS, 0), [("y", 0, 0), ("y", 0, 1), ("out", 0, 0)])])
        FIRST, PRE = plan_items(unit_groups(0, True))
        FIRST_ITEMS = [item for place in sorted(FIRST) for item in FIRST[place]]
        assert PER[0] % 2 == 0 and PRE[0] % 2 == 0

        def base(b, which):
            return 0 if b is None else PRE[which] + PER[which] * b

        def unit_after(g):
            nxt = (g + 1) % KV_HEADS
            return nxt, nxt % 2

        block = ctx.enter_context(nc.Block())

        @block.sync
        def _(sp):
            sp.dma_start(wk_raw[:], wk_in.rearrange("d (g c e) -> d g c e", g=KV_HEADS, c=2)).then_inc(w_in, 16)
            sp.dma_start(wv_raw[:], wv_in).then_inc(w_in, 16)
            sp.dma_start(wq_raw[:], wq_in).then_inc(w_in, 16)
            sp.dma_start(wo[:], wo_in.rearrange("(n p) d -> p n d", p=P)).then_inc(w_in, 16)

            def maxima(slot):
                sp.dma_start(q_max[slot][HEAD:HEAD + 1, :, :].bitcast(F32).rearrange("o j (t s) -> o (j t) s", s=P),
                             max_rows[:, slot, :].bitcast(F32)).then_inc(max_in, 16)

            sp.wait_ge(act_read, PRE[2])
            maxima(0)
            with sp.Fori(0, BATCH) as b:
                for g in range(KV_HEADS):
                    last = [i for s in range(NS) for i in BODY.get((g, s), []) if i.kind == "maxT"][0]
                    sp.wait_ge(act_read, base(b, 2) + last.act)
                    maxima(unit_after(g)[1])
            sp.wait_ge(max_in, 16 * (KV_HEADS * BATCH + 1))

        @block.gpsimd
        def _(pool):
            nc.gpsimd.memset(ident[:], 0.0).then_inc(consts, 1)
            nc.gpsimd.memset(ident_b[:], 0.0).then_inc(consts, 1)
            nc.gpsimd.memset(mask_q[:], 0.0).then_inc(consts, 1)
            nc.gpsimd.memset(mask_k[:], 0.0).then_inc(consts, 1)
            nc.gpsimd.memset(minus_half[:], -0.5).then_inc(consts, 1)
            pool.wait_ge(consts, 5)
            for m in (ident, ident_b):
                nc.gpsimd.affine_select(out=m[:], in_=m[:], compare_op=ALU.not_equal, fill=1.0, base=0,
                                        pattern=[[-1, P]], channel_multiplier=1).then_inc(consts, 1)
            nc.gpsimd.affine_select(out=mask_q[:], in_=mask_q[:], compare_op=ALU.is_ge, fill=STRUCK, base=0,
                                    pattern=[[-1, P]], channel_multiplier=1).then_inc(consts, 1)
            nc.gpsimd.affine_select(out=mask_k[:], in_=mask_k[:], compare_op=ALU.is_ge, fill=STRUCK, base=0,
                                    pattern=[[1, P]], channel_multiplier=-1).then_inc(consts, 1)

            def rstd_of(batch):
                pool.wait_ge(var_ready, batch + 1)
                nc.gpsimd.tensor_tensor(rstd[:], var_eps[:], minus_half[:], ALU.pow).then_inc(rstd_ready, 1)

            rstd_of(0)
            with pool.Fori(0, BATCH) as b:
                rstd_of(b + 1)

        @block.scalar
        def _(act):
            def read(item, b, slot, g):
                src = ps_i[item.slot]
                if item.kind in ("peak", "out"):
                    return
                act.wait_ge(item_done, base(b, 0) + item.done)
                if item.kind == "xT":
                    nc.scalar.activation(xT_hi[:], src[:], ACT.Copy).then_inc(hi_ready, 1)
                elif item.kind == "K":
                    nc.scalar.activation(k_twice[slot][:], src[:], ACT.Copy).then_inc(hi_ready, 1)
                elif item.kind == "V":
                    nc.scalar.activation(v_ones[slot][:, :, 0:HEAD],
                                         src[:, 0:ST * HEAD].rearrange("p (t d) -> p t d", t=ST),
                                         ACT.Copy).then_inc(act_read, 1)
                elif item.kind == "Q":
                    for n, dst in ((0, q_both), (1, q_both), (0, q_max), (1, q_max)):
                        last = nc.scalar.activation(dst[slot][0:HEAD, item.head + n, :],
                                                    src[n * HEAD:(n + 1) * HEAD, :], ACT.Copy)
                    last.then_inc(hi_ready, 1)
                elif item.kind == "maxT":
                    nc.scalar.activation(max_rows[:, slot, :], src[0:QPK * ST, 0:P], ACT.Copy).then_inc(act_read, 1)
                elif item.kind == "y":
                    nc.scalar.activation(yT[:, item.tile * CHUNK:(item.tile + 1) * CHUNK], src[:, 0:CHUNK],
                                         ACT.Copy).then_inc(act_read, 1)

            act.wait_ge(w_in, 64)
            nc.scalar.activation(wk_hi[:], wk_raw[:], ACT.Copy)
            nc.scalar.activation(wv_hi[:], wv_raw[:], ACT.Copy)
            nc.scalar.activation(wq_hi[:], wq_raw[:], ACT.Copy).then_inc(w_upper, 1)
            for item in FIRST_ITEMS:
                read(item, None, 0, 0)
            with act.Fori(0, BATCH) as b:
                for g in range(KV_HEADS):
                    for s, (j, qc, kt) in enumerate(STEPS):
                        n = g * NS + s
                        width = CHUNK - cols_of(qc, kt)[1]
                        act.wait_ge(s_done, KV_HEADS * NS * b + (n + 1))
                        if n >= 4:
                            act.wait_ge(pv_done, KV_HEADS * NS * b + (n - 3))
                        nc.scalar.activation(probs[:, s % 4, 0:width], ps_s[s % 2][:, 0:width], ACT.Exp,
                                             scale=SCALE).then_inc(exp_done, 1)
                        for item in BODY.get((g, s), []):
                            read(item, b, unit_after(g)[1], g)
                for item in BODY[(KV_HEADS, 0)]:
                    read(item, b, 0, 0)

        @block.vector
        def _(dve):
            def norm(batch):
                chain = Chain(dve, prep, 5 * batch)
                if isinstance(batch, int):
                    rows = x_rows[:, TPC + batch * ST:TPC + (batch + 1) * ST, :]
                else:
                    rows = x_rows[:, bass.ds(batch * ST + TPC, ST), :]

                def over(stat):
                    return stat[:].unsqueeze(2).to_broadcast([P, ST, P])

                chain.link(nc.vector.tensor_reduce(row_sum[:], rows, AX.X, ALU.add))
                chain.link(nc.vector.tensor_scalar(mean[:], row_sum[:], 1.0 / P, None, ALU.mult))
                chain.link(nc.vector.tensor_tensor(centred[:], rows, over(mean), ALU.subtract))
                chain.link(nc.vector.tensor_tensor(squares[:], centred[:], centred[:], ALU.mult))
                chain.link(nc.vector.tensor_reduce(sq_sum[:], squares[:], AX.X, ALU.add))
                nc.vector.tensor_scalar(var_eps[:], sq_sum[:], 1.0 / P, EPS, ALU.mult, ALU.add).then_inc(var_ready, 1)
                dve.wait_ge(rstd_ready, batch + 1)
                nc.vector.tensor_tensor(centred[:], centred[:], over(rstd), ALU.mult).then_inc(xn_ready, 1)

            def lower(out, item, b, src, hi):
                dve.wait_ge(hi_ready, base(b, 1) + item.hi)
                return nc.vector.tensor_tensor(out, src, hi.bitcast(F32), ALU.subtract)

            def read(item, b, slot, g):
                src = ps_i[item.slot]
                if item.kind == "xT":
                    lower(xT_lo[:], item, b, src[:], xT_hi[:]).then_inc(dve_read, 1)
                elif item.kind == "K":
                    lower(k_low[slot][0:HEAD, :], item, b, src[0:HEAD, :],
                          k_twice[slot][0:HEAD, :]).then_inc(dve_read, 1)
                elif item.kind == "Q":
                    for n in range(2):
                        last = lower(q_both[slot][HEAD:2 * HEAD, item.head + n, :], item, b,
                                     src[n * HEAD:(n + 1) * HEAD, :], q_both[slot][0:HEAD, item.head + n, :])
                    last.then_inc(dve_read, 1)
                elif item.kind == "peak":
                    dve.wait_ge(item_done, base(b, 0) + item.done)
                    at = item.head * ST + item.tile
                    nc.vector.tensor_reduce(neg_max[:, slot, at:at + 1], src[:, 0:(item.tile + 1) * P], AX.X, ALU.max,
                                            negate=True).then_inc(dve_read, 1)
                elif item.kind == "out":
                    dve.wait_ge(item_done, base(b, 0) + item.done)
                    rows = x_rows[:, bass.ds(b * ST + TPC, ST), :]
                    nc.vector.tensor_tensor(rows, rows, src[:].rearrange("p (t d) -> p t d", t=ST),
                                            ALU.add).then_inc(dve_read, 1)

            def finish_head(b, g, j, qc):
                n = g * CHUNKS_U + j * QC + qc
                done = g * NS + STEPS.index((j, qc, (qc + 1) * TPC - 1)) + 1
                dve.wait_ge(pv_done, KV_HEADS * NS * b + done)
                src = ps_v[n % 2]
                nc.vector.reciprocal(inverse[:, n % 2, :], src[HEAD:2 * HEAD, :]).then_inc(inv_done, 1)
                dve.wait_ge(inv_done, KV_HEADS * CHUNKS_U * b + (n + 1))
                head = g * QPK + j
                side = slice((head % 2) * HEAD, (head % 2 + 1) * HEAD)
                nc.vector.tensor_tensor(oT[side, head // 2, qc * CHUNK:(qc + 1) * CHUNK], src[0:HEAD, :],
                                        inverse[:, n % 2, :], ALU.mult).then_inc(head_done, 1)

            for slot in range(2):
                nc.vector.memset(v_ones[slot][:, :, HEAD:], 1.0)
                nc.vector.memset(k_low[slot][HEAD:HEAD + 1, :].bitcast(F32), 1.0)
            nc.vector.memset(x_rows[:, TPC + BATCH * ST:, :], 0.0)
            norm(0)
            dve.wait_ge(w_upper, 1)
            nc.vector.tensor_tensor(wk_lo[:], wk_raw[:], wk_hi[:].bitcast(F32), ALU.subtract)
            nc.vector.tensor_tensor(wv_lo[:], wv_raw[:], wv_hi[:].bitcast(F32), ALU.subtract)
            nc.vector.tensor_tensor(wq_lo[:], wq_raw[:], wq_hi[:].bitcast(F32), ALU.subtract).then_inc(w_lower, 1)
            for item in FIRST_ITEMS:
                read(item, None, 0, 0)
            with dve.Fori(0, BATCH) as b:
                for g in range(KV_HEADS):
                    for s, (j, qc, kt) in enumerate(STEPS):
                        for item in BODY.get((g, s), []):
                            read(item, b, unit_after(g)[1], g)
                        if s >= LAG + 1:
                            dj, dqc, dkt = STEPS[s - LAG - 1]
                            if dkt == (dqc + 1) * TPC - 1:
                                finish_head(b, g, dj, dqc)
                    finish_head(b, g, QPK - 1, QC - 1)
                    if g == KV_HEADS - 2:
                        norm(b + 1)
                for item in BODY[(KV_HEADS, 0)]:
                    read(item, b, 0, 0)

        @block.tensor
        def _(pe):
            def split_product(out, w_h, w_l, x_h, x_l):
                nc.tensor.matmul(out, w_h, x_h, start=True, stop=False)
                nc.tensor.matmul(out, w_h, x_l, start=False, stop=False)
                return nc.tensor.matmul(out, w_l, x_h, start=False, stop=True)

            def write(item, b, slot, g):
                if item.two_before is None:
                    if b is not None:
                        pe.wait_ge(act_read, base(b, 2))
                        pe.wait_ge(dve_read, base(b, 3))
                elif item.two_before.last_is_act:
                    pe.wait_ge(act_read, base(b, 2) + item.two_before.act)
                else:
                    pe.wait_ge(dve_read, base(b, 3) + item.two_before.dve)
                dst = ps_i[item.slot]
                halves = [slice(c * CHUNK, (c + 1) * CHUNK) for c in range(QC)]
                if item.kind == "xT":
                    pe.wait_ge(xn_ready, 1 if b is None else b + 2)
                    for t in range(ST):
                        last = nc.tensor.transpose(dst[:, t * P:(t + 1) * P], centred[:, t, :], ident[:])
                elif item.kind == "K":
                    if item.two_before is None or item.two_before.kind != "x":
                        pe.wait_ge(dve_read, base(b, 3) + (item.dve - 1))
                    for c in halves:
                        last = split_product(dst[:, c], wk_hi[:, g, :, :].rearrange("p c e -> p (c e)"),
                                             wk_lo[:, g, :, :].rearrange("p c e -> p (c e)"), xT_hi[:, c], xT_lo[:, c])
                elif item.kind == "V":
                    gs = slice(g * HEAD, (g + 1) * HEAD)
                    for t in range(ST):
                        out, ts = dst[:, t * HEAD:(t + 1) * HEAD], slice(t * P, (t + 1) * P)
                        nc.tensor.matmul(out, xT_hi[:, ts], wv_hi[:, gs], start=True, stop=False)
                        nc.tensor.matmul(out, xT_hi[:, ts], wv_lo[:, gs], start=False, stop=False)
                        last = nc.tensor.matmul(out, xT_lo[:, ts], wv_hi[:, gs], start=False, stop=True)
                elif item.kind == "Q":
                    hs = slice((g * QPK + item.head) * HEAD, (g * QPK + item.head + 2) * HEAD)
                    for c in halves:
                        last = split_product(dst[:, c], wq_hi[:, hs], wq_lo[:, hs], xT_hi[:, c], xT_lo[:, c])
                elif item.kind == "peak":
                    if item.head == 0 and item.tile == 0:
                        pe.wait_ge(hi_ready, base(b, 1) + item.hi)
                    j, t = item.head, item.tile
                    query = q_max[slot][0:HEAD, j, t * P:(t + 1) * P]
                    for c in range(t // TPC + 1):
                        end = min((c + 1) * CHUNK, (t + 1) * P)
                        own = c == t // TPC
                        nc.tensor.matmul(dst[:, c * CHUNK:end], query, k_twice[slot][0:HEAD, c * CHUNK:end],
                                         start=True, stop=not own)
                    last = nc.tensor.matmul(dst[:, t * P:(t + 1) * P], ident_b[:], mask_q[:], start=False, stop=True)
                elif item.kind == "maxT":
                    pe.wait_ge(dve_read, base(b, 3) + item.dve)
                    last = nc.tensor.transpose(dst[0:QPK * ST, 0:P], neg_max[:, slot, :], ident[:])
                elif item.kind == "y":
                    c = halves[item.tile]
                    for pair in range(PAIRS):
                        heads = KV_HEADS * CHUNKS_U - (0 if item.tile else 1)
                        if pair >= PAIRS - 2:
                            pe.wait_ge(head_done, KV_HEADS * CHUNKS_U * b
                                       + (heads if pair == PAIRS - 1 else heads - 2 * QC))
                        last = nc.tensor.matmul(dst[:, 0:CHUNK], wo[:, pair, :], oT[:, pair, c], start=(pair == 0),
                                                stop=(pair == PAIRS - 1))
                elif item.kind == "out":
                    pe.wait_ge(act_read, base(b, 2) + item.act)
                    for t in range(ST):
                        last = nc.tensor.transpose(dst[:, t * P:(t + 1) * P], yT[:, t * P:(t + 1) * P], ident[:])
                last.then_inc(item_done, 1)

            def scores(b, g, s):
                j, qc, kt = STEPS[s]
                n = g * NS + s
                slot = g % 2
                first, offset = cols_of(qc, kt)
                width = CHUNK - offset
                keys = slice(kt * P, (kt + 1) * P)
                queries = slice(first, first + width)
                if n >= 2:
                    pe.wait_ge(exp_done, KV_HEADS * NS * b + (n - 1))
                if s == 0:
                    pe.wait_ge(max_in, 16 * KV_HEADS * b + 16 * (g + 1))
                out = ps_s[s % 2][:, 0:width]
                diagonal = first == kt * P
                nc.tensor.matmul(out, k_twice[slot][:, keys], q_both[slot][:, j, queries], start=True, stop=False)
                last = nc.tensor.matmul(out, k_low[slot][0:HEAD + 1, keys], q_max[slot][0:HEAD + 1, j, queries],
                                        start=False, stop=not diagonal)
                if diagonal:
                    last = nc.tensor.matmul(out[:, 0:P], ident_b[:], mask_k[:], start=False, stop=True)
                last.then_inc(s_done, 1)

            def values(b, g, s):
                j, qc, kt = STEPS[s]
                n = g * NS + s
                chunk = g * CHUNKS_U + j * QC + qc
                offset = cols_of(qc, kt)[1]
                if kt == 0 and chunk >= 2:
                    pe.wait_ge(head_done, KV_HEADS * CHUNKS_U * b + (chunk - 1))
                pe.wait_ge(exp_done, KV_HEADS * NS * b + (n + 1))
                nc.tensor.matmul(ps_v[chunk % 2][:, offset:], v_ones[g % 2][:, kt, :], probs[:, s % 4, 0:CHUNK - offset],
                                 start=(kt == 0), stop=(kt == (qc + 1) * TPC - 1)).then_inc(pv_done, 1)

            pe.wait_ge(consts, 9)
            pe.wait_ge(w_lower, 1)
            for item in FIRST_ITEMS:
                write(item, None, 0, 0)
            with pe.Fori(0, BATCH) as b:
                for g in range(KV_HEADS):
                    for s in range(NS):
                        scores(b, g, s)
                        for item in BODY.get((g, s), []):
                            write(item, b, unit_after(g)[1], unit_after(g)[0])
                        if s >= LAG:
                            values(b, g, s - LAG)
                    for s in range(NS - LAG, NS):
                        values(b, g, s)
                for item in BODY[(KV_HEADS, 0)]:
                    write(item, b, 0, 0)


def macaron_kernel(nc, x_in, wq_in, wk_in, wv_in, wo_in, wr_in, w1_in, b1_in, w2_in, b2_in, x_out):
    rows_in = x_in.rearrange("(c t p) d -> c p t d", t=TPC, p=P)
    rows_out = x_out.rearrange("(c t p) d -> c p t d", t=TPC, p=P)
    with ExitStack() as ctx:
        x_rows = ctx.enter_context(nc.sbuf_tensor("x_rows", [P, TPC + TOKENS // P + IDLE, P], F32))

        def load_x(sp, loaded):
            for c in range(CHUNKS):
                sp.dma_start(x_rows[:, (c + 1) * TPC:(c + 2) * TPC, :], rows_in[c]).then_inc(loaded, 16)

        def store_x(sp, c, stored):
            sp.dma_start(rows_out[bass.ds(c, 1)].rearrange("o p t d -> (o p) t d"),
                         x_rows[:, bass.ds((c + 1) * TPC, TPC), :]).then_inc(stored, 16)

        ffn_phase(nc, "f1", x_rows, w1_in, w2_in, b1_in, b2_in, wr_in, load_x=load_x)
        attention_phase(nc, x_rows, wq_in, wk_in, wv_in, wo_in)
        ffn_phase(nc, "f2", x_rows, w1_in, w2_in, b1_in, b2_in, wr_in, store_x=store_x)


def kernel(L0_attn_hidden_states, L0_attn_Wq, L0_attn_Wk, L0_attn_Wv, L0_attn_Wo, L0_ffn_Wr, L0_ffn_W1, L0_ffn_b1,
           L0_ffn_W2, L0_ffn_b2):
    import concourse.bacc as bacc
    import numpy as np
    from concourse.bass_utils import run_bass_kernel_spmd

    keys = np.asarray(L0_attn_Wk).T.reshape(P, KV_HEADS, 1, HEAD)
    arrays = {
        "in_x": np.asarray(L0_attn_hidden_states).reshape(TOKENS, P),
        "in_wq": np.asarray(L0_attn_Wq).T,
        "in_wk": np.concatenate([keys, keys], axis=2).reshape(P, KV_HEADS * 2 * HEAD),
        "in_wv": np.asarray(L0_attn_Wv).T,
        "in_wo": np.asarray(L0_attn_Wo).T,
        "in_wr": np.asarray(L0_ffn_Wr),
        "in_w1": np.asarray(L0_ffn_W1),
        "in_b1": np.asarray(L0_ffn_b1).reshape(EXPERTS * FSL, P).T,
        "in_w2": np.asarray(L0_ffn_W2),
        "in_b2": np.asarray(L0_ffn_b2).T,
    }
    arrays = {name: np.ascontiguousarray(a) for name, a in arrays.items()}
    nc = bacc.Bacc("TRN2", target_bir_lowering=False, num_devices=1)
    aps = [nc.dram_tensor(name, a.shape, F32, kind="ExternalInput").ap() for name, a in arrays.items()]
    out = nc.dram_tensor("out_x", (TOKENS, P), F32, kind="ExternalOutput").ap()
    macaron_kernel(nc, *aps, out)
    result = run_bass_kernel_spmd(nc, [arrays], core_ids=[0]).results[0]["out_x"]
    return result.reshape(BATCH, SEQ, P)
```

```python
from contextlib import ExitStack

import concourse.bass as bass
from concourse import mybir

ALU = mybir.AluOpType
ACT = mybir.ActivationFunctionType
AX = mybir.AxisListType
F32 = mybir.dt.float32
F32R = mybir.dt.float32r
BF16 = mybir.dt.bfloat16

P = 128
BATCH, SEQ = 4, 1024
TOKENS = BATCH * SEQ
CHUNK = 512
TPC = CHUNK // P
CHUNKS = TOKENS // CHUNK
EXPERTS, FF, TOP_K = 8, 512, 2
FSL = FF // P
HEADS, KV_HEADS, HEAD = 16, 4, 64
QPK = HEADS // KV_HEADS
EPS = 1e-5
STRUCK = -1e30
IDLE = SEQ // P

class Chain:

    def __init__(self, engine, sem, base):
        self.engine, self.sem, self.base, self.n = engine, sem, base, 0

    def step(self, instruction):
        self.n += 1
        instruction.then_inc(self.sem, 1)

    def after(self):
        self.engine.wait_ge(self.sem, self.base + self.n)

def ffn_phase(nc, tag, x_rows, w1_in, w2_in, b1_in, b2_in, wr_in, load_x=None, store_x=None):
    HSTEPS = EXPERTS * FSL
    SLOTS = 8
    LAG = 4
    ADDS = EXPERTS - 1
    PREP = 20
    RAW = 4
    with ExitStack() as ctx:
        def sb(name, shape, dt=F32):
            return ctx.enter_context(nc.sbuf_tensor(f"{name}_{tag}", shape, dt))

        def psum(name):
            return ctx.enter_context(nc.psum_tensor(f"{name}_{tag}", [P, CHUNK], F32))

        def sem(name):
            return ctx.enter_context(nc.semaphore(f"{name}_{tag}"))

        w1_raw = sb("w1_raw", [P, RAW, FF])
        w2_raw = sb("w2_raw", [P, RAW, FF])
        w1_hi = sb("w1_hi", [P, EXPERTS, FF], F32R)
        w1_lo = sb("w1_lo", [P, EXPERTS, FF], F32R)
        w2_hi = sb("w2_hi", [P, EXPERTS, FF], F32R)
        w2_lo = sb("w2_lo", [P, EXPERTS, FF], F32R)
        b1 = sb("b1", [P, EXPERTS * FSL])
        b2 = sb("b2", [P, EXPERTS])
        wr_raw = sb("wr_raw", [P, EXPERTS])
        wr_parts = sb("wr_parts", [P, 2 * EXPERTS], F32R)
        ident = sb("ident", [P, P])
        spread = sb("spread", [2 * EXPERTS, EXPERTS, P])
        spread_r = sb("spread_r", [2 * EXPERTS, EXPERTS, P], F32R)
        earlier = sb("earlier", [P, EXPERTS, EXPERTS])
        minus_half = sb("minus_half", [P, TPC])
        row_sum = sb("row_sum", [P, TPC])
        mean = sb("mean", [P, TPC])
        centred = sb("centred", [P, TPC, P])
        sq_sum = sb("sq_sum", [P, TPC])
        var_eps = sb("var_eps", [P, TPC])
        rstd = sb("rstd", [P, TPC])
        xn = sb("xn", [P, TPC, P])
        xT_hi = sb("xT_hi", [P, 2, CHUNK], F32R)
        xT_lo = sb("xT_lo", [P, 2, CHUNK], F32R)
        part = sb("part", [P, TPC, 2 * EXPERTS])
        logits = sb("logits", [P, TPC, EXPERTS])
        top = sb("top", [P, TPC])
        shifted = sb("shifted", [P, TPC, EXPERTS])
        weight = sb("weight", [P, TPC, EXPERTS])
        above = sb("above", [P, TPC, EXPERTS, EXPERTS])
        equal = sb("equal", [P, TPC, EXPERTS, EXPERTS])
        rank = sb("rank", [P, TPC, EXPERTS])
        chosen = sb("chosen", [P, TPC, EXPERTS])
        picked = sb("picked", [P, TPC, EXPERTS])
        pair_sum = sb("pair_sum", [P, TPC])
        twice_sum = sb("twice_sum", [P, TPC])
        inverse = sb("inverse", [P, TPC])
        gate = sb("gate", [P, TPC, EXPERTS])
        gate_hi = sb("gate_hi", [P, TPC, EXPERTS], F32R)
        gate_parts = sb("gate_parts", [P, TPC, 2 * EXPERTS])
        gateT = sb("gateT", [2 * EXPERTS, 2, CHUNK], F32R)
        h = sb("h", [P, SLOTS, CHUNK])
        h_hi = sb("h_hi", [P, SLOTS, CHUNK], F32R)
        h_lo = sb("h_lo", [P, SLOTS, CHUNK], F32R)
        gate_all = sb("gate_all", [P, 2, CHUNK])
        gated = sb("gated", [P, 2, CHUNK])
        acc = sb("acc", [P, CHUNK])

        ps_t = psum("ps_t")
        ps_g = psum("ps_g")
        ps_h = [psum(f"ps_h{i}") for i in range(4)]
        ps_y = [psum("ps_y0"), psum("ps_y1")]

        rows_in = sem("rows_in")
        small_in = sem("small_in")
        w_in = [sem(f"w_in{i}") for i in range(EXPERTS)]
        consts = sem("consts")
        wr_upper = sem("wr_upper")
        wr_lower = sem("wr_lower")
        spread_set = sem("spread_set")
        w1_upper = sem("w1_upper")
        w1_lower = sem("w1_lower")
        w2_upper = sem("w2_upper")
        w2_lower = sem("w2_lower")
        prep = sem("prep")
        var_ready = sem("var_ready")
        rstd_ready = sem("rstd_ready")
        xn_ready = sem("xn_ready")
        xT_done = sem("xT_done")
        xhi_ready = sem("xhi_ready")
        xlo_ready = sem("xlo_ready")
        logits_done = sem("logits_done")
        shift_ready = sem("shift_ready")
        exp_ready = sem("exp_ready")
        gate_ready = sem("gate_ready")
        gateT_done = sem("gateT_done")
        gateT_ready = sem("gateT_ready")
        spread_done = sem("spread_done")
        spread_ready = sem("spread_ready")
        h_done = sem("h_done")
        relu_done = sem("relu_done")
        hhi_ready = sem("hhi_ready")
        hlo_even = sem("hlo_even")
        hlo_odd = sem("hlo_odd")
        h_used = sem("h_used")
        gated_ready = sem("gated_ready")
        acc_done = sem("acc_done")
        outT_done = sem("outT_done")
        x_updated = sem("x_updated")
        stored = sem("stored")

        def wait_hlo(engine, c, n):
            engine.wait_ge(hlo_odd if n % 2 else hlo_even, HSTEPS // 2 * c + (n // 2 + 1))

        block = ctx.enter_context(nc.Block())

        @block.sync
        def _(sp):
            if load_x is not None:
                load_x(sp, rows_in)
            sp.dma_start(wr_raw[:], wr_in).then_inc(small_in, 16)
            sp.dma_start(b1[:], b1_in).then_inc(small_in, 16)
            sp.dma_start(b2[:], b2_in).then_inc(small_in, 16)
            for e in range(EXPERTS):
                if e >= RAW:
                    sp.wait_ge(w1_lower, e - RAW + 1)
                    sp.wait_ge(w2_lower, e - RAW + 1)
                sp.dma_start(w1_raw[:, e % RAW, :], w1_in[e]).then_inc(w_in[e], 16)
                sp.dma_start(w2_raw[:, e % RAW, :].rearrange("p (f d) -> p f d", f=FSL),
                             w2_in[e].rearrange("(f p) d -> p f d", p=P)).then_inc(w_in[e], 16)
            if store_x is not None:
                with sp.Fori(0, CHUNKS) as c:
                    sp.wait_ge(x_updated, c + 2)
                    store_x(sp, c, stored)
                sp.wait_ge(stored, 16 * CHUNKS)

        @block.gpsimd
        def _(pool):
            nc.gpsimd.memset(ident[:], 0.0).then_inc(consts, 1)
            nc.gpsimd.memset(spread[:], 0.0).then_inc(consts, 1)
            nc.gpsimd.memset(earlier[:], 0.0).then_inc(consts, 1)
            nc.gpsimd.memset(minus_half[:], -0.5).then_inc(consts, 1)
            pool.wait_ge(consts, 4)
            nc.gpsimd.affine_select(out=ident[:], in_=ident[:], compare_op=ALU.not_equal, fill=1.0, base=0,
                                    pattern=[[-1, P]], channel_multiplier=1).then_inc(consts, 1)
            nc.gpsimd.affine_select(out=spread[:], in_=spread[:], compare_op=ALU.not_equal, fill=1.0, base=0,
                                    pattern=[[-1, EXPERTS], [0, P]], channel_multiplier=1).then_inc(consts, 1)
            nc.gpsimd.affine_select(out=earlier[:], in_=earlier[:], compare_op=ALU.is_ge, fill=1.0, base=0,
                                    pattern=[[-1, EXPERTS], [1, EXPERTS]], channel_multiplier=0).then_inc(consts, 1)
            pool.wait_ge(consts, 7)
            nc.gpsimd.affine_select(out=spread[:], in_=spread[:], compare_op=ALU.not_equal, fill=1.0,
                                    base=-EXPERTS, pattern=[[-1, EXPERTS], [0, P]],
                                    channel_multiplier=1).then_inc(consts, 1)
            nc.gpsimd.memset(acc[:], 0.0).then_inc(acc_done, 1)

            def rstd_of(k):
                pool.wait_ge(var_ready, k + 1)
                nc.gpsimd.tensor_tensor(rstd[:], var_eps[:], minus_half[:], ALU.pow).then_inc(rstd_ready, 1)

            def add_up(c, e):
                pool.wait_ge(gated_ready, EXPERTS * c + (e + 3))
                if e == 1:
                    pool.wait_ge(outT_done, c + 1)
                    first = gated[:, 0, :]
                else:
                    pool.wait_ge(acc_done, ADDS * c + e)
                    first = acc[:]
                nc.gpsimd.tensor_tensor(acc[:], first, gated[:, e % 2, :], ALU.add).then_inc(acc_done, 1)

            rstd_of(0)
            for e in range(EXPERTS):
                pool.wait_ge(w2_upper, e + 1)
                nc.gpsimd.tensor_tensor(w2_lo[:, e, :], w2_raw[:, e % RAW, :], w2_hi[:, e, :].bitcast(F32),
                                        ALU.subtract).then_inc(w2_lower, 1)
            with pool.Fori(0, CHUNKS) as c:
                for n in range(HSTEPS):
                    if n % 2:
                        pool.wait_ge(hhi_ready, HSTEPS * c + (n + 1))
                        nc.gpsimd.tensor_tensor(h_lo[:, n % SLOTS, :], h[:, n % SLOTS, :], h_hi[:, n % SLOTS, :].bitcast(F32),
                                                ALU.subtract).then_inc(hlo_odd, 1)
                    if n == 5:
                        rstd_of(c + 1)
                    if n >= 14 and n % FSL == 2:
                        add_up(c, (n - 10) // FSL)
                add_up(c, EXPERTS - 2)
                add_up(c, EXPERTS - 1)

        @block.scalar
        def _(act):
            def transpose_hi(k, slot):
                act.wait_ge(xT_done, k + 1)
                nc.scalar.activation(xT_hi[:, slot, :], ps_t[:], ACT.Copy).then_inc(xhi_ready, 1)

            def exp_of(k):
                act.wait_ge(shift_ready, k + 1)
                nc.scalar.activation(weight[:], shifted[:], ACT.Exp).then_inc(exp_ready, 1)

            def gateT_of(k, slot):
                act.wait_ge(gateT_done, k + 1)
                nc.scalar.activation(gateT[:, slot, :], ps_t[0:2 * EXPERTS, :], ACT.Copy).then_inc(gateT_ready, 1)

            act.wait_ge(small_in, 48)
            nc.scalar.activation(wr_parts[:, 0:EXPERTS], wr_raw[:], ACT.Copy).then_inc(wr_upper, 1)
            act.wait_ge(consts, 8)
            nc.scalar.activation(spread_r[:], spread[:], ACT.Copy).then_inc(spread_set, 1)
            transpose_hi(0, 0)
            exp_of(0)
            for e in range(EXPERTS):
                act.wait_ge(w_in[e], 32)
                nc.scalar.activation(w1_hi[:, e, :], w1_raw[:, e % RAW, :], ACT.Copy).then_inc(w1_upper, 1)
                if e == 0:
                    gateT_of(0, 0)
            with act.Fori(0, CHUNKS // 2) as pair:
                for half in range(2):
                    c = 2 * pair + half
                    for n in range(HSTEPS):
                        e, f = divmod(n, FSL)
                        if f == 2:
                            act.wait_ge(spread_done, EXPERTS * c + (e + 1))
                            act.wait_ge(gated_ready, EXPERTS * c + (e + 1))
                            nc.scalar.activation(gate_all[:, e % 2, :], ps_g[:], ACT.Copy).then_inc(spread_ready, 1)
                        act.wait_ge(h_done, HSTEPS * c + (n + 1))
                        if n >= SLOTS:
                            wait_hlo(act, c, n - SLOTS)
                        nc.scalar.activation(h[:, n % SLOTS, :], ps_h[n % 4][:], ACT.Relu,
                                             bias=b1[:, n:n + 1]).then_inc(relu_done, 1)
                        if n == 11:
                            transpose_hi(c + 1, 1 - half)
                        if n == 21:
                            exp_of(c + 1)
                        if n == 30:
                            gateT_of(c + 1, 1 - half)

        @block.vector
        def _(dve):
            def rows_at(slot):
                if isinstance(slot, int):
                    return x_rows[:, slot * TPC:(slot + 1) * TPC, :]
                return x_rows[:, bass.ds(slot * TPC, TPC), :]

            def over(stat, width):
                return stat[:].unsqueeze(2).to_broadcast([P, TPC, width])

            class Prepare:

                def __init__(self, k, slot):
                    self.k, self.slot, self.chain = k, slot, Chain(dve, prep, PREP * k)

                def sum_rows(self):
                    self.chain.step(nc.vector.tensor_reduce(row_sum[:], rows_at(self.k + 1), AX.X, ALU.add))

                def mean_of_rows(self):
                    self.chain.after()
                    self.chain.step(nc.vector.tensor_scalar(mean[:], row_sum[:], 1.0 / P, None, ALU.mult))

                def centre(self):
                    self.chain.after()
                    self.chain.step(nc.vector.tensor_tensor(centred[:], rows_at(self.k + 1), over(mean, P),
                                                            ALU.subtract))

                def square(self):
                    self.chain.after()
                    self.chain.step(nc.vector.tensor_tensor(xn[:], centred[:], centred[:], ALU.mult))

                def sum_squares(self):
                    self.chain.after()
                    self.chain.step(nc.vector.tensor_reduce(sq_sum[:], xn[:], AX.X, ALU.add))

                def variance(self):
                    self.chain.after()
                    nc.vector.tensor_scalar(var_eps[:], sq_sum[:], 1.0 / P, EPS, ALU.mult,
                                            ALU.add).then_inc(var_ready, 1)

                def scale(self):
                    dve.wait_ge(rstd_ready, self.k + 1)
                    nc.vector.tensor_tensor(xn[:], centred[:], over(rstd, P), ALU.mult).then_inc(xn_ready, 1)

                def lower(self):
                    dve.wait_ge(xhi_ready, self.k + 1)
                    nc.vector.tensor_tensor(xT_lo[:, self.slot, :], ps_t[:], xT_hi[:, self.slot, :].bitcast(F32),
                                            ALU.subtract).then_inc(xlo_ready, 1)

                def read_logits(self):
                    dve.wait_ge(logits_done, self.k + 1)
                    self.chain.step(nc.vector.tensor_copy(
                        part[:], ps_t[:, 0:TPC * 2 * EXPERTS].rearrange("p (t e) -> p t e", t=TPC)))

                def add_logits(self):
                    self.chain.after()
                    self.chain.step(nc.vector.tensor_tensor(logits[:], part[:, :, 0:EXPERTS], part[:, :, EXPERTS:],
                                                            ALU.add))

                def top_logit(self):
                    self.chain.after()
                    self.chain.step(nc.vector.tensor_reduce(top[:], logits[:], AX.X, ALU.max))

                def shift(self):
                    self.chain.after()
                    nc.vector.tensor_tensor(shifted[:], logits[:], over(top, EXPERTS),
                                            ALU.subtract).then_inc(shift_ready, 1)

                def compare(self):
                    square = [P, TPC, EXPERTS, EXPERTS]
                    one = logits[:].unsqueeze(3).to_broadcast(square)
                    other = logits[:].unsqueeze(2).to_broadcast(square)
                    self.chain.step(nc.vector.tensor_tensor(equal[:], other, one, ALU.is_equal))
                    self.chain.step(nc.vector.tensor_tensor(above[:], other, one, ALU.is_gt))

                def equal_before(self):
                    before = earlier[:].unsqueeze(1).to_broadcast([P, TPC, EXPERTS, EXPERTS])
                    self.chain.after()
                    self.chain.step(nc.vector.tensor_tensor(equal[:], equal[:], before, ALU.mult))

                def join_ranks(self):
                    self.chain.after()
                    self.chain.step(nc.vector.tensor_tensor(above[:], above[:], equal[:], ALU.add))

                def sum_ranks(self):
                    self.chain.after()
                    self.chain.step(nc.vector.tensor_reduce(rank[:], above[:], AX.X, ALU.add))

                def choose(self):
                    self.chain.after()
                    self.chain.step(nc.vector.tensor_scalar(chosen[:], rank[:], float(TOP_K), None, ALU.is_lt))

                def pick(self):
                    self.chain.after()
                    dve.wait_ge(exp_ready, self.k + 1)
                    self.chain.step(nc.vector.tensor_tensor(picked[:], weight[:], chosen[:], ALU.mult))

                def sum_picked(self):
                    self.chain.after()
                    self.chain.step(nc.vector.tensor_reduce(pair_sum[:], picked[:], AX.X, ALU.add))

                def invert(self):
                    self.chain.after()
                    self.chain.step(nc.vector.tensor_scalar(twice_sum[:], pair_sum[:], 2.0, None, ALU.mult))
                    self.chain.after()
                    self.chain.step(nc.vector.reciprocal(inverse[:], twice_sum[:]))

                def gates(self):
                    self.chain.after()
                    self.chain.step(nc.vector.tensor_tensor(gate[:], picked[:], over(inverse, EXPERTS), ALU.mult))

                def gates_upper(self):
                    self.chain.after()
                    self.chain.step(nc.vector.tensor_copy(gate_hi[:], gate[:]))

                def gates_apart(self):
                    self.chain.after()
                    nc.vector.tensor_copy(gate_parts[:, :, 0:EXPERTS], gate_hi[:].bitcast(F32))
                    nc.vector.tensor_tensor(gate_parts[:, :, EXPERTS:], gate[:], gate_hi[:].bitcast(F32),
                                            ALU.subtract).then_inc(gate_ready, 1)
                    assert self.chain.n == PREP, self.chain.n

            AT = {0: (Prepare.sum_rows,), 1: (Prepare.mean_of_rows,), 2: (Prepare.centre,), 3: (Prepare.square,),
                  4: (Prepare.sum_squares,), 5: (Prepare.variance,), 8: (Prepare.scale,), 13: (Prepare.lower,),
                  17: (Prepare.read_logits,), 18: (Prepare.add_logits,), 19: (Prepare.top_logit, Prepare.shift),
                  20: (Prepare.compare,), 21: (Prepare.equal_before,), 22: (Prepare.join_ranks,),
                  23: (Prepare.sum_ranks,), 24: (Prepare.choose, Prepare.pick), 25: (Prepare.sum_picked,),
                  26: (Prepare.invert,), 27: (Prepare.gates, Prepare.gates_upper), 28: (Prepare.gates_apart,)}

            def gate_y(c, e):
                dve.wait_ge(h_used, HSTEPS * c + FSL * (e + 1))
                dve.wait_ge(spread_ready, EXPERTS * c + (e + 1))
                if e >= 2:
                    dve.wait_ge(acc_done, ADDS * c + (1 + max(e - 2, 1)))
                nc.vector.scalar_tensor_tensor(out=gated[:, e % 2, :], in0=ps_y[e % 2][:], scalar=b2[:, e:e + 1],
                                               in1=gate_all[:, e % 2, :], op0=ALU.add,
                                               op1=ALU.mult).then_inc(gated_ready, 1)

            def add_rows(slot):
                rows = rows_at(slot)
                nc.vector.tensor_tensor(rows, rows, ps_t[:].rearrange("p (t d) -> p t d", t=TPC),
                                        ALU.add).then_inc(x_updated, 1)

            nc.vector.memset(x_rows[:, 0:TPC, :], 0.0).then_inc(gated_ready, 1)
            nc.vector.memset(x_rows[:, (CHUNKS + 1) * TPC:, :], 0.0).then_inc(gated_ready, 1)
            if load_x is not None:
                dve.wait_ge(rows_in, 16 * CHUNKS)
            dve.wait_ge(wr_upper, 1)
            nc.vector.tensor_tensor(wr_parts[:, EXPERTS:], wr_raw[:], wr_parts[:, 0:EXPERTS].bitcast(F32),
                                    ALU.subtract).then_inc(wr_lower, 1)
            dve.wait_ge(consts, 8)
            chunk = Prepare(0, 0)
            for n in sorted(AT):
                for stage in AT[n]:
                    stage(chunk)
            for e in range(EXPERTS):
                dve.wait_ge(w1_upper, e + 1)
                nc.vector.tensor_copy(w2_hi[:, e, :], w2_raw[:, e % RAW, :]).then_inc(w2_upper, 1)
                nc.vector.tensor_tensor(w1_lo[:, e, :], w1_raw[:, e % RAW, :], w1_hi[:, e, :].bitcast(F32),
                                        ALU.subtract).then_inc(w1_lower, 1)

            with dve.Fori(0, CHUNKS // 2) as pair:
                for half in range(2):
                    c = 2 * pair + half
                    following = Prepare(c + 1, 1 - half)
                    for n in range(HSTEPS):
                        dve.wait_ge(relu_done, HSTEPS * c + (n + 1))
                        if n >= SLOTS:
                            dve.wait_ge(h_used, HSTEPS * c + (n - SLOTS + 1))
                        nc.vector.tensor_copy(h_hi[:, n % SLOTS, :], h[:, n % SLOTS, :]).then_inc(hhi_ready, 1)
                        if n % 2:
                            m = n - 1
                            dve.wait_ge(hhi_ready, HSTEPS * c + (m + 1))
                            nc.vector.tensor_tensor(h_lo[:, m % SLOTS, :], h[:, m % SLOTS, :], h_hi[:, m % SLOTS, :].bitcast(F32),
                                                    ALU.subtract).then_inc(hlo_even, 1)
                        for stage in AT.get(n, ()):
                            stage(following)
                        if n == 6:
                            dve.wait_ge(outT_done, c + 1)
                            add_rows(c)
                        if n >= LAG + FSL - 1 and (n - LAG) % FSL == FSL - 1:
                            gate_y(c, (n - LAG) // FSL)
                    gate_y(c, EXPERTS - 1)
            dve.wait_ge(outT_done, CHUNKS + 1)
            add_rows(CHUNKS)

        @block.tensor
        def _(pe):
            def transpose_rows(k):
                pe.wait_ge(xn_ready, k + 1)
                for t in range(TPC):
                    last = nc.tensor.transpose(ps_t[:, t * P:(t + 1) * P], xn[:, t, :], ident[:])
                last.then_inc(xT_done, 1)

            def logits_of(k, slot):
                pe.wait_ge(xlo_ready, k + 1)
                for t in range(TPC):
                    out = ps_t[:, t * 2 * EXPERTS:(t + 1) * 2 * EXPERTS]
                    cols = slice(t * P, (t + 1) * P)
                    nc.tensor.matmul(out, xT_hi[:, slot, cols], wr_parts[:], start=True, stop=False)
                    last = nc.tensor.matmul(out, xT_lo[:, slot, cols], wr_parts[:], start=False, stop=True)
                last.then_inc(logits_done, 1)

            def transpose_gates(k):
                pe.wait_ge(gate_ready, k + 1)
                for t in range(TPC):
                    last = nc.tensor.transpose(ps_t[0:2 * EXPERTS, t * P:(t + 1) * P], gate_parts[:, t, :], ident[:])
                last.then_inc(gateT_done, 1)

            def transpose_sum(done):
                pe.wait_ge(acc_done, done)
                for t in range(TPC):
                    last = nc.tensor.transpose(ps_t[:, t * P:(t + 1) * P], acc[:, t * P:(t + 1) * P], ident[:])
                last.then_inc(outT_done, 1)

            pe.wait_ge(consts, 8)
            transpose_rows(0)
            pe.wait_ge(wr_lower, 1)
            logits_of(0, 0)
            transpose_gates(0)
            pe.wait_ge(spread_set, 1)
            pe.wait_ge(w1_lower, 1)
            with pe.Fori(0, CHUNKS // 2) as pair:
                for half in range(2):
                    c = 2 * pair + half
                    for n in range(HSTEPS + LAG):
                        if n < HSTEPS:
                            e, f = divmod(n, FSL)
                            if f == 0:
                                if e == 0:
                                    pe.wait_ge(gateT_ready, c + 1)
                                else:
                                    pe.wait_ge(spread_ready, EXPERTS * c + e)
                                    pe.wait_ge(w1_lower, e + 1)
                                nc.tensor.matmul(ps_g[:], spread_r[:, e, :], gateT[:, half, :], start=True,
                                                 stop=True).then_inc(spread_done, 1)
                            if n >= 4:
                                pe.wait_ge(relu_done, HSTEPS * c + (n - 3))
                            fs = slice(f * P, (f + 1) * P)
                            nc.tensor.matmul(ps_h[n % 4][:], w1_hi[:, e, fs], xT_hi[:, half, :], start=True, stop=False)
                            nc.tensor.matmul(ps_h[n % 4][:], w1_hi[:, e, fs], xT_lo[:, half, :], start=False, stop=False)
                            nc.tensor.matmul(ps_h[n % 4][:], w1_lo[:, e, fs], xT_hi[:, half, :], start=False,
                                             stop=True).then_inc(h_done, 1)
                        if n == 4:
                            transpose_sum(ADDS * c + 1)
                        if n == 9:
                            pe.wait_ge(x_updated, c + 1)
                            transpose_rows(c + 1)
                        if n == 15:
                            logits_of(c + 1, 1 - half)
                        if n == 29:
                            transpose_gates(c + 1)
                        if n >= LAG:
                            m = n - LAG
                            e, f = divmod(m, FSL)
                            fs = slice(f * P, (f + 1) * P)
                            if f == 0:
                                pe.wait_ge(gated_ready, EXPERTS * c + (e + 1))
                            if f == 0:
                                pe.wait_ge(w2_lower, e + 1)
                            wait_hlo(pe, c, m)
                            y = ps_y[e % 2][:]
                            nc.tensor.matmul(y, w2_hi[:, e, fs], h_hi[:, m % SLOTS, :], start=(f == 0), stop=False)
                            nc.tensor.matmul(y, w2_hi[:, e, fs], h_lo[:, m % SLOTS, :], start=False, stop=False)
                            last = nc.tensor.matmul(y, w2_lo[:, e, fs], h_hi[:, m % SLOTS, :], start=False,
                                                    stop=(f == FSL - 1))
                            last.then_inc(h_used, 1)
            transpose_sum(ADDS * CHUNKS + 1)

class Item:

    def __init__(self, kind, slot, before, head=0, tile=0):
        self.kind, self.slot, self.head, self.tile = kind, slot, head, tile
        self.done = before[0] + 1
        self.hi = before[1] + {"xT": 1, "K": 1, "Q": 2}.get(kind, 0)
        self.act = before[2] + (kind in ("V", "maxT"))
        self.dve = before[3] + (kind in ("xT", "K", "Q", "peak", "out"))
        self.last_is_act = self.act > before[2]

def plan_items(groups):
    count, total, placed = (0, 0, 0, 0), 0, {}
    flat = []
    for place, kinds in groups:
        for kind, head, tile in kinds:
            item = Item(kind, total % 2, count, head, tile)
            count = (item.done, item.hi, item.act, item.dve)
            total += 1
            item.two_before = flat[-2] if len(flat) >= 2 else None
            flat.append(item)
            placed.setdefault(place, []).append(item)
    return placed, count

def attention_phase(nc, x_rows, wq_in, wk_in, wv_in, wo_in, inv_dram):
    with ExitStack() as ctx:
        def sb(name, shape, dt=F32):
            return ctx.enter_context(nc.sbuf_tensor(name, shape, dt))

        def psum(name, width=CHUNK):
            return ctx.enter_context(nc.psum_tensor(name, [P, width], F32))

        def sem(name):
            return ctx.enter_context(nc.semaphore(name))

        SCALE = float(HEAD) ** -0.5
        FRONT = ST = SEQ // P
        VT = TPC
        QC = SEQ // CHUNK
        PAIRS = HEADS // 2
        LAG = 3
        RING = LAG + 1

        wq_hi = sb("wq_hi", [P, HEADS * HEAD], F32R)
        wq_lo = sb("wq_lo", [P, HEADS * HEAD], F32R)
        wk_hi = sb("wk_hi", [P, KV_HEADS, 2, HEAD], F32R)
        wk_lo = sb("wk_lo", [P, KV_HEADS, 2, HEAD], F32R)
        wv_hi = sb("wv_hi", [P, KV_HEADS * HEAD], F32R)
        wv_lo = sb("wv_lo", [P, KV_HEADS * HEAD], F32R)
        wo = sb("wo", [P, PAIRS, P])
        ident = sb("ident_a", [P, P])
        ident_b = sb("ident_b", [P, P], BF16)
        mask_q = sb("mask_q", [P, P], BF16)
        mask_k = sb("mask_k", [P, P], BF16)
        minus_half = sb("minus_half_a", [P, ST])
        row_sum = sb("row_sum_a", [P, ST])
        mean = sb("mean_a", [P, ST])
        sq_sum = sb("sq_sum_a", [P, ST])
        var_eps = sb("var_eps_a", [P, ST])
        rstd = sb("rstd_a", [P, ST])
        centred = sb("centred_a", [P, ST, P])
        xT_hi = sb("xT_hi_a", [P, SEQ], F32R)
        xT_lo = sb("xT_lo_a", [P, SEQ], F32R)
        q_both = [sb(f"q_both{i}", [P, QPK, SEQ], F32R) for i in range(2)]
        q_max = [sb(f"q_max{i}", [P, QPK, SEQ], F32R) for i in range(2)]
        k_twice = [sb(f"k_twice{i}", [P, SEQ], F32R) for i in range(2)]
        k_low = [sb(f"k_low{i}", [P, SEQ], F32R) for i in range(2)]
        v_raw = sb("v_raw", [P, ST, KV_HEADS * HEAD])
        v_hi = [sb(f"v_hi{i}", [P, ST, HEAD + 2], F32R) for i in range(2)]
        v_lo = [sb(f"v_lo{i}", [P, ST, HEAD], F32R) for i in range(2)]
        neg_max = sb("neg_max", [P, 2, QPK * ST])
        max_rows = sb("max_rows", [QPK * ST, 2, P], F32R)
        probs = sb("probs", [P, RING, CHUNK])
        probs_hi = sb("probs_hi", [P, RING, CHUNK], F32R)
        probs_lo = sb("probs_lo", [P, RING, CHUNK], F32R)
        sums = sb("sums", [1, SEQ])
        sums_t = sb("sums_t", [P, 2, ST])
        inv_t = sb("inv_t", [P, 2, ST])
        inv_all = sb("inv_all", [P, 2, SEQ])
        oT = sb("oT", [P, 4, SEQ])
        wq_raw = oT[:, 0, :]
        wk_raw = oT[:, 1, 0:KV_HEADS * 2 * HEAD].rearrange("d (g c e) -> d g c e", g=KV_HEADS, c=2)
        wv_raw = oT[:, 2, 0:KV_HEADS * HEAD]
        squares = v_raw[:, :, 0:P]

        ps_s = [psum("ps_s0"), psum("ps_s1")]
        ps_v = [psum("ps_v0"), psum("ps_v1")]
        ps_i = [psum("ps_i0", 2 * CHUNK), psum("ps_i1", 2 * CHUNK)]

        w_in = sem("w_in_a")
        consts = sem("consts_a")
        w_upper = sem("w_upper_a")
        w_lower = sem("w_lower_a")
        prep = sem("prep_a")
        var_ready = sem("var_ready_a")
        rstd_ready = sem("rstd_ready_a")
        xn_ready = sem("xn_ready_a")
        item_done = sem("item_done")
        hi_ready = sem("hi_ready")
        act_read = sem("act_read")
        dve_read = sem("dve_read")
        max_in = sem("max_in")
        v_upper = sem("v_upper")
        v_lower = sem("v_lower")
        lo_done = sem("lo_done")
        q_twice = sem("q_twice")
        s_done = sem("s_done")
        exp_done = sem("exp_done")
        pv_done = sem("pv_done")
        copied = sem("copied")
        sums_out = sem("sums_out")
        sums_in = sem("sums_in")
        inverted = sem("inverted")
        inv_out = sem("inv_out")
        inv_in = [sem("inv_in_even"), sem("inv_in_odd")]
        scaled = sem("scaled")

        ORDER = [[0, 3, 1, 2], [0, 7, 1, 6, 2, 5, 3, 4]]
        STEPS = [(j, qc, kt) for j in range(QPK) for qc in range(QC) for kt in ORDER[qc]]
        NS = len(STEPS)
        NB = KV_HEADS * NS
        CHUNKS_U = QPK * QC

        def cols_of(qc, kt):
            first = max(qc * CHUNK, kt * P)
            return first, first - qc * CHUNK

        def unit_groups(g, first, tail=()):
            late = 5 if first else 1
            groups = [(0, [("xT", 0, 0)]), (1, [("xT", 0, 1)]), (late + 1, [("V", 0, 0)]),
                      (late + 2, [("V", 0, 1)])] if first else []
            groups += [(late, [("K", 0, 0)]), (late + 3, [("Q", 0, 0)]), (late + 5, [("Q", 2, 0)])]
            place = late + 6
            for j in range(QPK):
                for tiles in ((0, 1), (2,), (3,), (4,), (5,), (6,), (7,)):
                    place += 1
                    groups += [(place, [("peak", j, t) for t in tiles])]
            groups += [(place + 4, [("maxT", 0, 0)])] + list(tail)
            assert place + 4 < NS
            return [((g, step), kinds) for step, kinds in sorted(groups, key=lambda group: group[0])]

        OUT = 18
        NORM = (KV_HEADS - 1) * NS - 4
        RSTD = NORM
        SPLIT = 9

        BODY, PER = plan_items([x for g in range(KV_HEADS)
                                for x in unit_groups(g, g == KV_HEADS - 1, [(OUT, [("out", g, 0)])])])
        FIRST, PRE = plan_items(unit_groups(0, True))
        FIRST_ITEMS = [item for place in sorted(FIRST) for item in FIRST[place]]
        FIRST_V, BODY_V = [max(item.act for items in plan.values() for item in items if item.kind == "V")
                           for plan in (FIRST, BODY)]
        SECOND = {(g, s + 1): [item for item in items if item.kind == "Q"] for (g, s), items in BODY.items()}
        LAST = plan_items([(0, [("out", 0, 0)])])[0][0][0]
        assert PER[0] % 2 == 0 and PRE[0] % 2 == 0

        def base(b, which):
            return 0 if b is None else PRE[which] + PER[which] * b

        def unit_after(g):
            nxt = (g + 1) % KV_HEADS
            return nxt, nxt % 2

        def steps_through(g, j, qc):
            return g * NS + STEPS.index((j, qc, ORDER[qc][-1])) + 1

        ENDED = {steps_through(g, j, qc) + LAG: (g, j, qc) for g in range(KV_HEADS) for j in range(QPK)
                 for qc in range(QC)}

        block = ctx.enter_context(nc.Block())

        @block.sync
        def _(sp):
            sp.dma_start(wk_raw, wk_in.rearrange("d (g c e) -> d g c e", g=KV_HEADS, c=2)).then_inc(w_in, 16)
            sp.dma_start(wv_raw, wv_in).then_inc(w_in, 16)
            sp.dma_start(wq_raw, wq_in).then_inc(w_in, 16)
            sp.dma_start(wo[:], wo_in.rearrange("(n p) d -> p n d", p=P)).then_inc(w_in, 16)

            with sp.Fori(0, BATCH) as b:
                for head in range(HEADS):
                    slot, pair, side = head % 2, head // 2, (head % 2) * HEAD
                    n = HEADS * b + head
                    sp.wait_ge(sums_out, 2 + QC * n + QC)
                    sp.dma_start(sums_t[:, slot, :], sums[:].rearrange("o (p t) -> o p t", t=ST)).then_inc(sums_in, 16)
                    sp.wait_ge(inverted, n + 1)
                    sp.dma_start(inv_dram[slot].rearrange("(p t) -> p t", t=ST), inv_t[:, slot, :]).then_inc(inv_out, 16)
                    sp.wait_ge(inv_out, 16 * n + 16)
                    sp.dma_start(inv_all[side:side + HEAD, pair % 2, :],
                                 inv_dram[slot:slot + 1, :].to_broadcast([HEAD, SEQ])).then_inc(inv_in[head % 2], 16)

        @block.gpsimd
        def _(pool):
            nc.gpsimd.memset(ident[:], 0.0).then_inc(consts, 1)
            nc.gpsimd.memset(ident_b[:], 0.0).then_inc(consts, 1)
            nc.gpsimd.memset(mask_q[:], 0.0).then_inc(consts, 1)
            nc.gpsimd.memset(mask_k[:], 0.0).then_inc(consts, 1)
            nc.gpsimd.memset(minus_half[:], -0.5).then_inc(consts, 1)
            pool.wait_ge(consts, 5)
            for m in (ident, ident_b):
                nc.gpsimd.affine_select(out=m[:], in_=m[:], compare_op=ALU.not_equal, fill=1.0, base=0,
                                        pattern=[[-1, P]], channel_multiplier=1).then_inc(consts, 1)
            nc.gpsimd.affine_select(out=mask_q[:], in_=mask_q[:], compare_op=ALU.is_ge, fill=STRUCK, base=0,
                                    pattern=[[-1, P]], channel_multiplier=1).then_inc(consts, 1)
            nc.gpsimd.affine_select(out=mask_k[:], in_=mask_k[:], compare_op=ALU.is_ge, fill=STRUCK, base=0,
                                    pattern=[[1, P]], channel_multiplier=-1).then_inc(consts, 1)

            def rstd_of(batch):
                pool.wait_ge(var_ready, batch + 1)
                nc.gpsimd.tensor_tensor(rstd[:], var_eps[:], minus_half[:], ALU.pow).then_inc(rstd_ready, 1)

            rstd_of(0)
            with pool.Fori(0, BATCH) as b:
                for n in range(NB):
                    if n == RSTD:
                        rstd_of(b + 1)
                    width = CHUNK - cols_of(*STEPS[n % NS][1:])[1]
                    pool.wait_ge(exp_done, NB * b + (n + 1))
                    nc.gpsimd.tensor_tensor(probs_lo[:, n % RING, 0:width], probs[:, n % RING, 0:width],
                                            probs_hi[:, n % RING, 0:width].bitcast(F32),
                                            ALU.subtract).then_inc(lo_done, 1)

        @block.scalar
        def _(act):
            def read(item, b, slot, g):
                src = ps_i[item.slot]
                if item.kind in ("peak", "out"):
                    return
                act.wait_ge(item_done, base(b, 0) + item.done)
                if item.kind == "xT":
                    half = slice(item.tile * CHUNK, (item.tile + 1) * CHUNK)
                    nc.scalar.activation(xT_hi[:, half], src[:, 0:CHUNK], ACT.Copy).then_inc(hi_ready, 1)
                elif item.kind == "K":
                    nc.scalar.activation(k_twice[slot][:], src[:], ACT.Copy).then_inc(hi_ready, 1)
                elif item.kind == "V":
                    nc.scalar.activation(v_raw[:, item.tile * VT:(item.tile + 1) * VT, :],
                                         src[:].rearrange("p (t d) -> p t d", t=VT), ACT.Copy).then_inc(act_read, 1)
                elif item.kind == "Q":
                    nc.scalar.activation(q_both[slot][0:HEAD, item.head, :], src[0:HEAD, :],
                                         ACT.Copy).then_inc(hi_ready, 1)
                elif item.kind == "maxT":
                    nc.scalar.activation(max_rows[:, slot, :], src[0:QPK * ST, 0:P], ACT.Copy).then_inc(act_read, 1)
                    act.wait_ge(act_read, base(b, 2) + item.act)
                    act.dma_start(q_max[slot][HEAD:HEAD + 1, :, :].bitcast(F32).rearrange("o j (t s) -> o (j t) s", s=P),
                                  max_rows[:, slot, :].bitcast(F32)).then_inc(max_in, 16)

            def read_second(item, slot):
                nc.scalar.activation(q_both[slot][0:HEAD, item.head + 1, :], ps_i[item.slot][HEAD:2 * HEAD, :],
                                     ACT.Copy).then_inc(hi_ready, 1)

            def upper_values(b, g, slot):
                act.wait_ge(act_read, base(b, 2) + (FIRST_V if b is None else BODY_V if g == 0 else 0))
                nc.scalar.activation(v_hi[slot][:, :, 0:HEAD], v_raw[:, :, g * HEAD:(g + 1) * HEAD],
                                     ACT.Copy).then_inc(v_upper, 1)

            def take_sums(b, g, j, qc):
                head, chunk = g * QPK + j, g * CHUNKS_U + j * QC + qc
                act.wait_ge(pv_done, NB * b + steps_through(g, j, qc))
                if head >= 1 and qc == 0:
                    act.wait_ge(sums_in, 16 * HEADS * b + 16 * head)
                nc.scalar.activation(sums[0:1, qc * CHUNK:(qc + 1) * CHUNK],
                                     ps_v[chunk % 2][HEAD:HEAD + 1, :], ACT.Copy).then_inc(sums_out, 1)

            act.wait_ge(w_in, 64)
            nc.scalar.activation(wk_hi[:], wk_raw, ACT.Copy)
            nc.scalar.activation(wv_hi[:], wv_raw, ACT.Copy).then_inc(sums_out, 2)
            nc.scalar.activation(wq_hi[:], wq_raw, ACT.Copy).then_inc(w_upper, 1)
            for item in FIRST_ITEMS:
                read(item, None, 0, 0)
                if item.kind == "Q":
                    read_second(item, 0)
            upper_values(None, 0, 0)
            with act.Fori(0, BATCH) as b:
                for n in range(NB):
                    g, s = n // NS, n % NS
                    width = CHUNK - cols_of(*STEPS[s][1:])[1]
                    act.wait_ge(s_done, NB * b + (n + 1))
                    nc.scalar.activation(probs[:, n % RING, 0:width], ps_s[n % 2][:, 0:width], ACT.Exp, scale=SCALE)
                    nc.scalar.activation(probs_hi[:, n % RING, 0:width], ps_s[n % 2][:, 0:width], ACT.Exp,
                                         scale=SCALE).then_inc(exp_done, 1)
                    for item in BODY.get((g, s), []):
                        read(item, b, unit_after(g)[1], g)
                    for item in SECOND.get((g, s), []):
                        read_second(item, unit_after(g)[1])
                    if s == SPLIT:
                        upper_values(b, *unit_after(g))
                    if n in ENDED:
                        take_sums(b, *ENDED[n])
                take_sums(b, KV_HEADS - 1, QPK - 1, QC - 1)
            act.wait_ge(max_in, 16 * (KV_HEADS * BATCH + 1))

        @block.vector
        def _(dve):
            def norm(batch):
                chain = Chain(dve, prep, 5 * batch)
                if isinstance(batch, int):
                    rows = x_rows[:, FRONT + batch * ST:FRONT + (batch + 1) * ST, :]
                else:
                    rows = x_rows[:, bass.ds(batch * ST + FRONT, ST), :]

                def over(stat):
                    return stat[:].unsqueeze(2).to_broadcast([P, ST, P])

                chain.step(nc.vector.tensor_reduce(row_sum[:], rows, AX.X, ALU.add))
                chain.after()
                chain.step(nc.vector.tensor_scalar(mean[:], row_sum[:], 1.0 / P, None, ALU.mult))
                chain.after()
                chain.step(nc.vector.tensor_tensor(centred[:], rows, over(mean), ALU.subtract))
                chain.after()
                chain.step(nc.vector.tensor_tensor(squares, centred[:], centred[:], ALU.mult))
                chain.after()
                chain.step(nc.vector.tensor_reduce(sq_sum[:], squares, AX.X, ALU.add))
                chain.after()
                nc.vector.tensor_scalar(var_eps[:], sq_sum[:], 1.0 / P, EPS, ALU.mult, ALU.add).then_inc(var_ready, 1)
                dve.wait_ge(rstd_ready, batch + 1)
                nc.vector.tensor_tensor(centred[:], centred[:], over(rstd), ALU.mult).then_inc(xn_ready, 1)

            def lower(out, item, b, src, hi):
                dve.wait_ge(hi_ready, base(b, 1) + item.hi)
                return nc.vector.tensor_tensor(out, src, hi.bitcast(F32), ALU.subtract)

            def read(item, b, slot, g):
                src = ps_i[item.slot]
                if item.kind == "xT":
                    half = slice(item.tile * CHUNK, (item.tile + 1) * CHUNK)
                    lower(xT_lo[:, half], item, b, src[:, 0:CHUNK], xT_hi[:, half]).then_inc(dve_read, 1)
                elif item.kind == "K":
                    lower(k_low[slot][0:HEAD, :], item, b, src[0:HEAD, :],
                          k_twice[slot][0:HEAD, :]).then_inc(dve_read, 1)
                elif item.kind == "Q":
                    read_head(item, b, slot, 0)
                elif item.kind == "peak":
                    dve.wait_ge(item_done, base(b, 0) + item.done)
                    at = item.head * ST + item.tile
                    nc.vector.tensor_reduce(neg_max[:, slot, at:at + 1], src[:, 0:(item.tile + 1) * P], AX.X, ALU.max,
                                            negate=True).then_inc(dve_read, 1)
                elif item.kind == "out":
                    dve.wait_ge(item_done, base(b, 0) + item.done)
                    shift = 0 if item.head == 0 else ST
                    rows = x_rows[:, bass.ds(b * ST + shift, ST), :] if not isinstance(b, int) else \
                        x_rows[:, b * ST + shift:(b + 1) * ST + shift, :]
                    nc.vector.tensor_tensor(rows, rows, src[:].rearrange("p (t d) -> p t d", t=ST),
                                            ALU.add).then_inc(dve_read, 1)

            def read_head(item, b, slot, n):
                upper = q_both[slot][0:HEAD, item.head + n, :]
                dve.wait_ge(hi_ready, base(b, 1) + item.hi - 1 + n)
                last = nc.vector.tensor_tensor(q_both[slot][HEAD:2 * HEAD, item.head + n, :],
                                               ps_i[item.slot][n * HEAD:(n + 1) * HEAD, :], upper.bitcast(F32),
                                               ALU.subtract)
                nc.vector.tensor_copy(q_max[slot][0:HEAD, item.head + n, :], upper).then_inc(q_twice, 1)
                if n == 1:
                    last.then_inc(dve_read, 1)

            def lower_values(b, g, slot):
                dve.wait_ge(v_upper, 1 if b is None else KV_HEADS * b + ((g - 1) % KV_HEADS + 2))
                nc.vector.tensor_tensor(v_lo[slot][:], v_raw[:, :, g * HEAD:(g + 1) * HEAD],
                                        v_hi[slot][:, :, 0:HEAD].bitcast(F32), ALU.subtract).then_inc(v_lower, 1)

            def take_values(b, g, j, qc):
                head, chunk = g * QPK + j, g * CHUNKS_U + j * QC + qc
                dve.wait_ge(pv_done, NB * b + steps_through(g, j, qc))
                side = slice((head % 2) * HEAD, (head % 2 + 1) * HEAD)
                nc.vector.tensor_copy(oT[side, head // 2 % 4, qc * CHUNK:(qc + 1) * CHUNK],
                                      ps_v[chunk % 2][0:HEAD, :]).then_inc(copied, 1)

            def invert_sums(b, head):
                dve.wait_ge(sums_in, 16 * HEADS * b + 16 * (head + 1))
                nc.vector.reciprocal(inv_t[:, head % 2, :], sums_t[:, head % 2, :]).then_inc(inverted, 1)

            def scale_pair(b, pair):
                for side in range(2):
                    dve.wait_ge(inv_in[side], 16 * PAIRS * b + 16 * (pair + 1))
                dve.wait_ge(copied, 2 + KV_HEADS * CHUNKS_U * b + QC * (2 * pair + 2))
                nc.vector.tensor_tensor(oT[:, pair % 4, :], oT[:, pair % 4, :], inv_all[:, pair % 2, :],
                                        ALU.mult).then_inc(scaled, 1)

            for slot in range(2):
                nc.vector.memset(v_hi[slot][:, :, HEAD:].bitcast(F32), 1.0)
                nc.vector.memset(k_low[slot][HEAD:HEAD + 1, :].bitcast(F32), 1.0)
            nc.vector.memset(x_rows[:, 0:FRONT, :], 0.0).then_inc(copied, 2)
            nc.vector.memset(x_rows[:, FRONT + BATCH * ST:, :], 0.0)
            norm(0)
            dve.wait_ge(w_upper, 1)
            nc.vector.tensor_tensor(wk_lo[:], wk_raw, wk_hi[:].bitcast(F32), ALU.subtract)
            nc.vector.tensor_tensor(wv_lo[:], wv_raw, wv_hi[:].bitcast(F32), ALU.subtract)
            nc.vector.tensor_tensor(wq_lo[:], wq_raw, wq_hi[:].bitcast(F32), ALU.subtract).then_inc(w_lower, 1)
            for item in FIRST_ITEMS:
                read(item, None, 0, 0)
                if item.kind == "Q":
                    read_head(item, None, 0, 1)
            lower_values(None, 0, 0)
            nc.vector.memset(oT[:, 2:4, :], 0.0).then_inc(scaled, 1)
            with dve.Fori(0, BATCH) as b:
                for n in range(NB):
                    g, s = n // NS, n % NS
                    if n == NORM:
                        norm(b + 1)
                    for item in BODY.get((g, s), []):
                        read(item, b, unit_after(g)[1], g)
                    for item in SECOND.get((g, s), []):
                        read_head(item, b, unit_after(g)[1], 1)
                    if s == SPLIT:
                        lower_values(b, *unit_after(g))
                    if n in ENDED:
                        take_values(b, *ENDED[n])
                    if s % 12 == 9:
                        head = g * QPK + s // 12 - 1
                        if head >= 0:
                            invert_sums(b, head)
                    if s in (17, 41):
                        pair = 2 * g + s // 24 - 1
                        if pair >= 0:
                            scale_pair(b, pair)
                take_values(b, KV_HEADS - 1, QPK - 1, QC - 1)
                invert_sums(b, HEADS - 1)
                scale_pair(b, PAIRS - 1)
            read(LAST, BATCH, 0, 0)

        @block.tensor
        def _(pe):
            def split_product(out, w_h, w_l, x_h, x_l):
                nc.tensor.matmul(out, w_h, x_h, start=True, stop=False)
                nc.tensor.matmul(out, w_h, x_l, start=False, stop=False)
                return nc.tensor.matmul(out, w_l, x_h, start=False, stop=True)

            def write(item, b, slot, g):
                if item.two_before is None:
                    if b is not None:
                        pe.wait_ge(act_read, base(b, 2))
                        pe.wait_ge(dve_read, base(b, 3))
                elif item.two_before.last_is_act:
                    pe.wait_ge(act_read, base(b, 2) + item.two_before.act)
                else:
                    pe.wait_ge(dve_read, base(b, 3) + item.two_before.dve)
                dst = ps_i[item.slot]
                halves = [slice(c * CHUNK, (c + 1) * CHUNK) for c in range(QC)]
                if item.kind == "xT":
                    pe.wait_ge(xn_ready, 1 if b is None else b + 2)
                    for t in range(TPC):
                        last = nc.tensor.transpose(dst[:, t * P:(t + 1) * P], centred[:, item.tile * TPC + t, :],
                                                   ident[:])
                elif item.kind == "K":
                    pe.wait_ge(dve_read, base(b, 3) + (item.dve - 1))
                    for c in halves:
                        last = split_product(dst[:, c], wk_hi[:, g, :, :].rearrange("p c e -> p (c e)"),
                                             wk_lo[:, g, :, :].rearrange("p c e -> p (c e)"), xT_hi[:, c], xT_lo[:, c])
                elif item.kind == "V":
                    for t in range(VT):
                        out = dst[:, t * KV_HEADS * HEAD:(t + 1) * KV_HEADS * HEAD]
                        ts = slice((item.tile * VT + t) * P, (item.tile * VT + t + 1) * P)
                        nc.tensor.matmul(out, xT_hi[:, ts], wv_hi[:], start=True, stop=False)
                        nc.tensor.matmul(out, xT_hi[:, ts], wv_lo[:], start=False, stop=False)
                        last = nc.tensor.matmul(out, xT_lo[:, ts], wv_hi[:], start=False, stop=True)
                elif item.kind == "Q":
                    hs = slice((g * QPK + item.head) * HEAD, (g * QPK + item.head + 2) * HEAD)
                    for c in halves:
                        last = split_product(dst[:, c], wq_hi[:, hs], wq_lo[:, hs], xT_hi[:, c], xT_lo[:, c])
                elif item.kind == "peak":
                    if item.head == 0 and item.tile == 0:
                        pe.wait_ge(dve_read, base(b, 3) + (item.dve - 1))
                    j, t = item.head, item.tile
                    query = q_both[slot][:, j, t * P:(t + 1) * P]
                    for c in range(t // TPC + 1):
                        end = min((c + 1) * CHUNK, (t + 1) * P)
                        own = c == t // TPC
                        nc.tensor.matmul(dst[:, c * CHUNK:end], query, k_twice[slot][:, c * CHUNK:end],
                                         start=True, stop=not own)
                    last = nc.tensor.matmul(dst[:, t * P:(t + 1) * P], ident_b[:], mask_q[:], start=False, stop=True)
                elif item.kind == "maxT":
                    pe.wait_ge(dve_read, base(b, 3) + item.dve)
                    last = nc.tensor.transpose(dst[0:QPK * ST, 0:P], neg_max[:, slot, :], ident[:])
                elif item.kind == "out":
                    pe.wait_ge(scaled, 1 + PAIRS * b + 2 * item.head)
                    pairs = [(2 * item.head - 2 + p) % PAIRS for p in range(2)]
                    for t in range(ST):
                        for pair in pairs:
                            last = nc.tensor.matmul(dst[:, t * P:(t + 1) * P], oT[:, pair % 4, t * P:(t + 1) * P],
                                                    wo[:, pair, :], start=(pair == pairs[0]), stop=(pair == pairs[1]))
                last.then_inc(item_done, 1)

            def scores(b, g, s):
                j, qc, kt = STEPS[s]
                slot = g % 2
                n = g * NS + s
                first, offset = cols_of(qc, kt)
                width = CHUNK - offset
                keys = slice(kt * P, (kt + 1) * P)
                queries = slice(first, first + width)
                if n >= 2:
                    pe.wait_ge(exp_done, NB * b + (n - 1))
                if s == 0:
                    pe.wait_ge(q_twice, QPK * KV_HEADS * b + QPK * (g + 1))
                    pe.wait_ge(max_in, 16 * KV_HEADS * b + 16 * (g + 1))
                out = ps_s[n % 2][:, 0:width]
                diagonal = first == kt * P
                nc.tensor.matmul(out, k_twice[slot][:, keys], q_both[slot][:, j, queries], start=True, stop=False)
                last = nc.tensor.matmul(out, k_low[slot][0:HEAD + 1, keys], q_max[slot][0:HEAD + 1, j, queries],
                                        start=False, stop=not diagonal)
                if diagonal:
                    last = nc.tensor.matmul(out[:, 0:P], ident_b[:], mask_k[:], start=False, stop=True)
                last.then_inc(s_done, 1)

            def values(b, g, s):
                j, qc, kt = STEPS[s]
                n = g * NS + s
                chunk = g * CHUNKS_U + j * QC + qc
                offset = cols_of(qc, kt)[1]
                if s == 0:
                    pe.wait_ge(v_lower, KV_HEADS * b + (g + 1))
                if kt == 0:
                    pe.wait_ge(copied, KV_HEADS * CHUNKS_U * b + (chunk + 1))
                    pe.wait_ge(sums_out, KV_HEADS * CHUNKS_U * b + (chunk + 1))
                pe.wait_ge(exp_done, NB * b + (n + 1))
                upper, lower = probs_hi[:, n % RING, 0:CHUNK - offset], probs_lo[:, n % RING, 0:CHUNK - offset]
                nc.tensor.matmul(ps_v[chunk % 2][0:HEAD + 2, offset:], v_hi[g % 2][:, kt, :], upper,
                                 start=(kt == 0), stop=False)
                nc.tensor.matmul(ps_v[chunk % 2][0:HEAD, offset:], v_lo[g % 2][:, kt, :], upper, start=False,
                                 stop=False)
                pe.wait_ge(lo_done, NB * b + (n + 1))
                nc.tensor.matmul(ps_v[chunk % 2][0:HEAD + 2, offset:], v_hi[g % 2][:, kt, :], lower, start=False,
                                 stop=(kt == ORDER[qc][-1])).then_inc(pv_done, 1)

            pe.wait_ge(consts, 9)
            pe.wait_ge(w_lower, 1)
            for item in FIRST_ITEMS:
                write(item, None, 0, 0)
            with pe.Fori(0, BATCH) as b:
                for n in range(NB):
                    g, s = n // NS, n % NS
                    scores(b, g, s)
                    for item in BODY.get((g, s), []):
                        write(item, b, unit_after(g)[1], unit_after(g)[0])
                    if n >= LAG:
                        values(b, (n - LAG) // NS, (n - LAG) % NS)
                for n in range(NB - LAG, NB):
                    values(b, n // NS, n % NS)
            write(LAST, BATCH, 0, 0)

def macaron_kernel(nc, x_in, wq_in, wk_in, wv_in, wo_in, wr_in, w1_in, b1_in, w2_in, b2_in, x_out):
    rows_in = x_in.rearrange("(c t p) d -> c p t d", t=TPC, p=P)
    rows_out = x_out.rearrange("(c t p) d -> c p t d", t=TPC, p=P)
    with ExitStack() as ctx:
        rows_all = ctx.enter_context(nc.sbuf_tensor("rows_all", [P, IDLE + TOKENS // P + IDLE, P], F32))
        x_rows = rows_all[:, IDLE - TPC:, :]

        def load_x(sp, loaded):
            for c in range(CHUNKS):
                sp.dma_start(x_rows[:, (c + 1) * TPC:(c + 2) * TPC, :], rows_in[c]).then_inc(loaded, 16)

        def store_x(sp, c, stored):
            sp.dma_start(rows_out[bass.ds(c, 1)].rearrange("o p t d -> (o p) t d"),
                         x_rows[:, bass.ds((c + 1) * TPC, TPC), :]).then_inc(stored, 16)

        ffn_phase(nc, "f1", x_rows, w1_in, w2_in, b1_in, b2_in, wr_in, load_x=load_x)
        inv_dram = nc.dram_tensor("inv_dram", (2, SEQ), F32, kind="Internal").ap()
        attention_phase(nc, rows_all, wq_in, wk_in, wv_in, wo_in, inv_dram)
        ffn_phase(nc, "f2", x_rows, w1_in, w2_in, b1_in, b2_in, wr_in, store_x=store_x)

def kernel(L0_attn_hidden_states, L0_attn_Wq, L0_attn_Wk, L0_attn_Wv, L0_attn_Wo, L0_ffn_Wr, L0_ffn_W1, L0_ffn_b1,
           L0_ffn_W2, L0_ffn_b2):
    import concourse.bacc as bacc
    import numpy as np
    from concourse.bass_utils import run_bass_kernel_spmd

    keys = np.asarray(L0_attn_Wk).T.reshape(P, KV_HEADS, 1, HEAD)
    arrays = {
        "in_x": np.asarray(L0_attn_hidden_states).reshape(TOKENS, P),
        "in_wq": np.asarray(L0_attn_Wq).T,
        "in_wk": np.concatenate([keys, keys], axis=2).reshape(P, KV_HEADS * 2 * HEAD),
        "in_wv": np.asarray(L0_attn_Wv).T,
        "in_wo": np.asarray(L0_attn_Wo).T,
        "in_wr": np.asarray(L0_ffn_Wr),
        "in_w1": np.asarray(L0_ffn_W1),
        "in_b1": np.asarray(L0_ffn_b1).reshape(EXPERTS * FSL, P).T,
        "in_w2": np.asarray(L0_ffn_W2),
        "in_b2": np.asarray(L0_ffn_b2).T,
    }
    arrays = {name: np.ascontiguousarray(a) for name, a in arrays.items()}
    nc = bacc.Bacc("TRN2", target_bir_lowering=False, num_devices=1)
    aps = [nc.dram_tensor(name, a.shape, F32, kind="ExternalInput").ap() for name, a in arrays.items()]
    out = nc.dram_tensor("out_x", (TOKENS, P), F32, kind="ExternalOutput").ap()
    macaron_kernel(nc, *aps, out)
    result = run_bass_kernel_spmd(nc, [arrays], core_ids=[0]).results[0]["out_x"]
    return result.reshape(BATCH, SEQ, P)
```

```python
from contextlib import ExitStack

import concourse.bass as bass
from concourse import mybir

ALU = mybir.AluOpType
ACT = mybir.ActivationFunctionType
AX = mybir.AxisListType
F32 = mybir.dt.float32
F32R = mybir.dt.float32r
BF16 = mybir.dt.bfloat16

P = 128
BATCH, SEQ = 4, 1024
TOKENS = BATCH * SEQ
CHUNK = 512
TPC = CHUNK // P
CHUNKS = TOKENS // CHUNK
EXPERTS, FF, TOP_K = 8, 512, 2
FSL = FF // P
HEADS, KV_HEADS, HEAD = 16, 4, 64
QPK = HEADS // KV_HEADS
EPS = 1e-5
STRUCK = -1e30
IDLE = SEQ // P

class Chain:

    def __init__(self, engine, sem, base):
        self.engine, self.sem, self.base, self.n = engine, sem, base, 0

    def step(self, instruction):
        self.n += 1
        instruction.then_inc(self.sem, 1)

    def after(self):
        self.engine.wait_ge(self.sem, self.base + self.n)

def ffn_phase(nc, tag, x_rows, w1_in, w2_in, b1_in, b2_in, wr_in, load_x=None, store_x=None):
    HSTEPS = EXPERTS * FSL
    SLOTS = 8
    LAG = 4
    ADDS = EXPERTS - 1
    PREP = 20
    RAW = 4
    with ExitStack() as ctx:
        def sb(name, shape, dt=F32):
            return ctx.enter_context(nc.sbuf_tensor(f"{name}_{tag}", shape, dt))

        def psum(name):
            return ctx.enter_context(nc.psum_tensor(f"{name}_{tag}", [P, CHUNK], F32))

        def sem(name):
            return ctx.enter_context(nc.semaphore(f"{name}_{tag}"))

        w1_raw = sb("w1_raw", [P, RAW, FF])
        w2_raw = sb("w2_raw", [P, RAW, FF])
        w1_hi = sb("w1_hi", [P, EXPERTS, FF], F32R)
        w1_lo = sb("w1_lo", [P, EXPERTS, FF], F32R)
        w2_hi = sb("w2_hi", [P, EXPERTS, FF], F32R)
        w2_lo = sb("w2_lo", [P, EXPERTS, FF], F32R)
        b1 = sb("b1", [P, EXPERTS * FSL])
        b2 = sb("b2", [P, EXPERTS])
        wr_raw = sb("wr_raw", [P, EXPERTS])
        wr_parts = sb("wr_parts", [P, 2 * EXPERTS], F32R)
        ident = sb("ident", [P, P])
        spread = sb("spread", [2 * EXPERTS, EXPERTS, P])
        spread_r = sb("spread_r", [2 * EXPERTS, EXPERTS, P], F32R)
        earlier = sb("earlier", [P, EXPERTS, EXPERTS])
        minus_half = sb("minus_half", [P, TPC])
        row_sum = sb("row_sum", [P, TPC])
        mean = sb("mean", [P, TPC])
        centred = sb("centred", [P, TPC, P])
        sq_sum = sb("sq_sum", [P, TPC])
        var_eps = sb("var_eps", [P, TPC])
        rstd = sb("rstd", [P, TPC])
        xn = sb("xn", [P, TPC, P])
        xT_hi = sb("xT_hi", [P, 2, CHUNK], F32R)
        xT_lo = sb("xT_lo", [P, 2, CHUNK], F32R)
        part = sb("part", [P, TPC, 2 * EXPERTS])
        logits = sb("logits", [P, TPC, EXPERTS])
        top = sb("top", [P, TPC])
        shifted = sb("shifted", [P, TPC, EXPERTS])
        weight = sb("weight", [P, TPC, EXPERTS])
        above = sb("above", [P, TPC, EXPERTS, EXPERTS])
        equal = sb("equal", [P, TPC, EXPERTS, EXPERTS])
        rank = sb("rank", [P, TPC, EXPERTS])
        chosen = sb("chosen", [P, TPC, EXPERTS])
        picked = sb("picked", [P, TPC, EXPERTS])
        pair_sum = sb("pair_sum", [P, TPC])
        twice_sum = sb("twice_sum", [P, TPC])
        inverse = sb("inverse", [P, TPC])
        gate = sb("gate", [P, TPC, EXPERTS])
        gate_hi = sb("gate_hi", [P, TPC, EXPERTS], F32R)
        gate_parts = sb("gate_parts", [P, TPC, 2 * EXPERTS])
        gateT = sb("gateT", [2 * EXPERTS, 2, CHUNK], F32R)
        h = sb("h", [P, SLOTS, CHUNK])
        h_hi = sb("h_hi", [P, SLOTS, CHUNK], F32R)
        h_lo = sb("h_lo", [P, SLOTS, CHUNK], F32R)
        gate_all = sb("gate_all", [P, 2, CHUNK])
        gated = sb("gated", [P, 2, CHUNK])
        acc = sb("acc", [P, CHUNK])

        ps_t = psum("ps_t")
        ps_g = psum("ps_g")
        ps_h = [psum(f"ps_h{i}") for i in range(4)]
        ps_y = [psum("ps_y0"), psum("ps_y1")]

        first_in = sem("first_in")
        rows_in = sem("rows_in")
        small_in = sem("small_in")
        w_in = [sem(f"w_in{i}") for i in range(EXPERTS)]
        consts = sem("consts")
        wr_upper = sem("wr_upper")
        wr_lower = sem("wr_lower")
        spread_set = sem("spread_set")
        w1_upper = sem("w1_upper")
        w1_lower = sem("w1_lower")
        w2_upper = sem("w2_upper")
        w2_lower = sem("w2_lower")
        prep = sem("prep")
        var_ready = sem("var_ready")
        rstd_ready = sem("rstd_ready")
        xn_ready = sem("xn_ready")
        xT_done = sem("xT_done")
        xhi_ready = sem("xhi_ready")
        xlo_ready = sem("xlo_ready")
        logits_done = sem("logits_done")
        shift_ready = sem("shift_ready")
        exp_ready = sem("exp_ready")
        gate_ready = sem("gate_ready")
        gateT_done = sem("gateT_done")
        gateT_ready = sem("gateT_ready")
        spread_done = sem("spread_done")
        spread_ready = sem("spread_ready")
        h_done = sem("h_done")
        relu_done = sem("relu_done")
        hhi_ready = sem("hhi_ready")
        hlo_even = sem("hlo_even")
        hlo_odd = sem("hlo_odd")
        h_used = sem("h_used")
        gated_ready = sem("gated_ready")
        acc_done = sem("acc_done")
        outT_done = sem("outT_done")
        x_updated = sem("x_updated")
        stored = sem("stored")

        def wait_hlo(engine, c, n):
            engine.wait_ge(hlo_odd if n % 2 else hlo_even, HSTEPS // 2 * c + (n // 2 + 1))

        block = ctx.enter_context(nc.Block())

        @block.sync
        def _(sp):
            if load_x is not None:
                load_x(sp, 0, first_in)
            sp.dma_start(wr_raw[:], wr_in).then_inc(small_in, 16)
            sp.dma_start(b1[:], b1_in).then_inc(small_in, 16)
            sp.dma_start(b2[:], b2_in).then_inc(small_in, 16)
            for e in range(EXPERTS):
                if e >= RAW:
                    sp.wait_ge(w1_lower, e - RAW + 1)
                    sp.wait_ge(w2_lower, e - RAW + 1)
                sp.dma_start(w1_raw[:, e % RAW, :], w1_in[e]).then_inc(w_in[e], 16)
                sp.dma_start(w2_raw[:, e % RAW, :].rearrange("p (f d) -> p f d", f=FSL),
                             w2_in[e].rearrange("(f p) d -> p f d", p=P)).then_inc(w_in[e], 16)
                if e == 0 and load_x is not None:
                    for c in range(1, CHUNKS):
                        load_x(sp, c, rows_in)
            if store_x is not None:
                with sp.Fori(0, CHUNKS) as c:
                    sp.wait_ge(x_updated, c + 2)
                    store_x(sp, c, stored)
                sp.wait_ge(stored, 16 * CHUNKS)

        @block.gpsimd
        def _(pool):
            nc.gpsimd.memset(ident[:], 0.0).then_inc(consts, 1)
            nc.gpsimd.memset(spread[:], 0.0).then_inc(consts, 1)
            nc.gpsimd.memset(earlier[:], 0.0).then_inc(consts, 1)
            nc.gpsimd.memset(minus_half[:], -0.5).then_inc(consts, 1)
            pool.wait_ge(consts, 4)
            nc.gpsimd.affine_select(out=ident[:], in_=ident[:], compare_op=ALU.not_equal, fill=1.0, base=0,
                                    pattern=[[-1, P]], channel_multiplier=1).then_inc(consts, 1)
            nc.gpsimd.affine_select(out=spread[:], in_=spread[:], compare_op=ALU.not_equal, fill=1.0, base=0,
                                    pattern=[[-1, EXPERTS], [0, P]], channel_multiplier=1).then_inc(consts, 1)
            nc.gpsimd.affine_select(out=earlier[:], in_=earlier[:], compare_op=ALU.is_ge, fill=1.0, base=0,
                                    pattern=[[-1, EXPERTS], [1, EXPERTS]], channel_multiplier=0).then_inc(consts, 1)
            pool.wait_ge(consts, 7)
            nc.gpsimd.affine_select(out=spread[:], in_=spread[:], compare_op=ALU.not_equal, fill=1.0,
                                    base=-EXPERTS, pattern=[[-1, EXPERTS], [0, P]],
                                    channel_multiplier=1).then_inc(consts, 1)
            nc.gpsimd.memset(acc[:], 0.0).then_inc(acc_done, 1)

            def rstd_of(k):
                pool.wait_ge(var_ready, k + 1)
                nc.gpsimd.tensor_tensor(rstd[:], var_eps[:], minus_half[:], ALU.pow).then_inc(rstd_ready, 1)

            def add_up(c, e):
                pool.wait_ge(gated_ready, EXPERTS * c + (e + 3))
                if e == 1:
                    pool.wait_ge(outT_done, c + 1)
                    first = gated[:, 0, :]
                else:
                    pool.wait_ge(acc_done, ADDS * c + e)
                    first = acc[:]
                nc.gpsimd.tensor_tensor(acc[:], first, gated[:, e % 2, :], ALU.add).then_inc(acc_done, 1)

            def split_w2(e):
                pool.wait_ge(w2_upper, e + 1)
                nc.gpsimd.tensor_tensor(w2_lo[:, e, :], w2_raw[:, e % RAW, :], w2_hi[:, e, :].bitcast(F32),
                                        ALU.subtract).then_inc(w2_lower, 1)

            def split_hidden(c, n):
                pool.wait_ge(hhi_ready, HSTEPS * c + (n + 1))
                nc.gpsimd.tensor_tensor(h_lo[:, n % SLOTS, :], h[:, n % SLOTS, :], h_hi[:, n % SLOTS, :].bitcast(F32),
                                        ALU.subtract).then_inc(hlo_odd, 1)

            rstd_of(0)
            split_w2(0)
            for n in range(1, LAG, 2):
                split_hidden(0, n)
            for e in range(1, EXPERTS):
                split_w2(e)
            with pool.Fori(0, CHUNKS) as c:
                for n in range(HSTEPS):
                    if n % 2:
                        split_hidden(c, n + LAG)
                    if n == 5:
                        rstd_of(c + 1)
                    if n >= FSL + 6 and n % FSL == 2:
                        add_up(c, (n - 6) // FSL)
                add_up(c, EXPERTS - 1)

        @block.scalar
        def _(act):
            def transpose_hi(k, slot):
                act.wait_ge(xT_done, k + 1)
                nc.scalar.activation(xT_hi[:, slot, :], ps_t[:], ACT.Copy).then_inc(xhi_ready, 1)

            def exp_of(k):
                act.wait_ge(shift_ready, k + 1)
                nc.scalar.activation(weight[:], shifted[:], ACT.Exp).then_inc(exp_ready, 1)

            def gateT_of(k, slot):
                act.wait_ge(gateT_done, k + 1)
                nc.scalar.activation(gateT[:, slot, :], ps_t[0:2 * EXPERTS, :], ACT.Copy).then_inc(gateT_ready, 1)

            def relu(c, n):
                act.wait_ge(h_done, HSTEPS * c + (n + 1))
                nc.scalar.activation(h[:, n % SLOTS, :], ps_h[n % 4][:], ACT.Relu,
                                     bias=b1[:, n % HSTEPS:n % HSTEPS + 1]).then_inc(relu_done, 1)

            def split_w1(e):
                act.wait_ge(w_in[e], 32)
                nc.scalar.activation(w1_hi[:, e, :], w1_raw[:, e % RAW, :], ACT.Copy).then_inc(w1_upper, 1)

            act.wait_ge(small_in, 48)
            nc.scalar.activation(wr_parts[:, 0:EXPERTS], wr_raw[:], ACT.Copy).then_inc(wr_upper, 1)
            split_w1(0)
            transpose_hi(0, 0)
            act.wait_ge(consts, 8)
            nc.scalar.activation(spread_r[:], spread[:], ACT.Copy).then_inc(spread_set, 1)
            exp_of(0)
            for n in range(LAG):
                relu(0, n)
            split_w1(1)
            gateT_of(0, 0)
            for e in range(2, EXPERTS):
                split_w1(e)
            with act.Fori(0, CHUNKS // 2) as pair:
                for half in range(2):
                    c = 2 * pair + half
                    for n in range(HSTEPS):
                        relu(c, n + LAG)
                        e, f = divmod(n, FSL)
                        if f == 1:
                            act.wait_ge(spread_done, EXPERTS * c + (e + 1))
                            act.wait_ge(gated_ready, EXPERTS * c + (e + 1))
                            nc.scalar.activation(gate_all[:, e % 2, :], ps_g[:], ACT.Copy).then_inc(spread_ready, 1)
                        if n == 11:
                            transpose_hi(c + 1, 1 - half)
                        if n == 21:
                            exp_of(c + 1)
                        if n == 30:
                            gateT_of(c + 1, 1 - half)

        @block.vector
        def _(dve):
            def rows_at(slot):
                if isinstance(slot, int):
                    return x_rows[:, slot * TPC:(slot + 1) * TPC, :]
                return x_rows[:, bass.ds(slot * TPC, TPC), :]

            def over(stat, width):
                return stat[:].unsqueeze(2).to_broadcast([P, TPC, width])

            class Prepare:

                def __init__(self, k, slot):
                    self.k, self.slot, self.chain = k, slot, Chain(dve, prep, PREP * k)

                def sum_rows(self):
                    self.chain.step(nc.vector.tensor_reduce(row_sum[:], rows_at(self.k + 1), AX.X, ALU.add))

                def mean_of_rows(self):
                    self.chain.after()
                    self.chain.step(nc.vector.tensor_scalar(mean[:], row_sum[:], 1.0 / P, None, ALU.mult))

                def centre(self):
                    self.chain.after()
                    self.chain.step(nc.vector.tensor_tensor(centred[:], rows_at(self.k + 1), over(mean, P),
                                                            ALU.subtract))

                def square(self):
                    self.chain.after()
                    self.chain.step(nc.vector.tensor_tensor(xn[:], centred[:], centred[:], ALU.mult))

                def sum_squares(self):
                    self.chain.after()
                    self.chain.step(nc.vector.tensor_reduce(sq_sum[:], xn[:], AX.X, ALU.add))

                def variance(self):
                    self.chain.after()
                    nc.vector.tensor_scalar(var_eps[:], sq_sum[:], 1.0 / P, EPS, ALU.mult,
                                            ALU.add).then_inc(var_ready, 1)

                def scale(self):
                    dve.wait_ge(rstd_ready, self.k + 1)
                    nc.vector.tensor_tensor(xn[:], centred[:], over(rstd, P), ALU.mult).then_inc(xn_ready, 1)

                def lower(self):
                    dve.wait_ge(xhi_ready, self.k + 1)
                    nc.vector.tensor_tensor(xT_lo[:, self.slot, :], ps_t[:], xT_hi[:, self.slot, :].bitcast(F32),
                                            ALU.subtract).then_inc(xlo_ready, 1)

                def read_logits(self):
                    dve.wait_ge(logits_done, self.k + 1)
                    self.chain.step(nc.vector.tensor_copy(
                        part[:], ps_t[:, 0:TPC * 2 * EXPERTS].rearrange("p (t e) -> p t e", t=TPC)))

                def add_logits(self):
                    self.chain.after()
                    self.chain.step(nc.vector.tensor_tensor(logits[:], part[:, :, 0:EXPERTS], part[:, :, EXPERTS:],
                                                            ALU.add))

                def top_logit(self):
                    self.chain.after()
                    self.chain.step(nc.vector.tensor_reduce(top[:], logits[:], AX.X, ALU.max))

                def shift(self):
                    self.chain.after()
                    nc.vector.tensor_tensor(shifted[:], logits[:], over(top, EXPERTS),
                                            ALU.subtract).then_inc(shift_ready, 1)

                def compare(self):
                    square = [P, TPC, EXPERTS, EXPERTS]
                    one = logits[:].unsqueeze(3).to_broadcast(square)
                    other = logits[:].unsqueeze(2).to_broadcast(square)
                    self.chain.step(nc.vector.tensor_tensor(equal[:], other, one, ALU.is_equal))
                    self.chain.step(nc.vector.tensor_tensor(above[:], other, one, ALU.is_gt))

                def equal_before(self):
                    before = earlier[:].unsqueeze(1).to_broadcast([P, TPC, EXPERTS, EXPERTS])
                    self.chain.after()
                    self.chain.step(nc.vector.tensor_tensor(equal[:], equal[:], before, ALU.mult))

                def join_ranks(self):
                    self.chain.after()
                    self.chain.step(nc.vector.tensor_tensor(above[:], above[:], equal[:], ALU.add))

                def sum_ranks(self):
                    self.chain.after()
                    self.chain.step(nc.vector.tensor_reduce(rank[:], above[:], AX.X, ALU.add))

                def choose(self):
                    self.chain.after()
                    self.chain.step(nc.vector.tensor_scalar(chosen[:], rank[:], float(TOP_K), None, ALU.is_lt))

                def pick(self):
                    self.chain.after()
                    dve.wait_ge(exp_ready, self.k + 1)
                    self.chain.step(nc.vector.tensor_tensor(picked[:], weight[:], chosen[:], ALU.mult))

                def sum_picked(self):
                    self.chain.after()
                    self.chain.step(nc.vector.tensor_reduce(pair_sum[:], picked[:], AX.X, ALU.add))

                def invert(self):
                    self.chain.after()
                    self.chain.step(nc.vector.tensor_scalar(twice_sum[:], pair_sum[:], 2.0, None, ALU.mult))
                    self.chain.after()
                    self.chain.step(nc.vector.reciprocal(inverse[:], twice_sum[:]))

                def gates(self):
                    self.chain.after()
                    self.chain.step(nc.vector.tensor_tensor(gate[:], picked[:], over(inverse, EXPERTS), ALU.mult))

                def gates_upper(self):
                    self.chain.after()
                    self.chain.step(nc.vector.tensor_copy(gate_hi[:], gate[:]))

                def gates_apart(self):
                    self.chain.after()
                    nc.vector.tensor_copy(gate_parts[:, :, 0:EXPERTS], gate_hi[:].bitcast(F32))
                    nc.vector.tensor_tensor(gate_parts[:, :, EXPERTS:], gate[:], gate_hi[:].bitcast(F32),
                                            ALU.subtract).then_inc(gate_ready, 1)
                    assert self.chain.n == PREP, self.chain.n

            AT = {0: (Prepare.sum_rows,), 1: (Prepare.mean_of_rows,), 2: (Prepare.centre,), 3: (Prepare.square,),
                  4: (Prepare.sum_squares,), 5: (Prepare.variance,), 8: (Prepare.scale,), 13: (Prepare.lower,),
                  17: (Prepare.read_logits,), 18: (Prepare.add_logits,), 19: (Prepare.top_logit, Prepare.shift),
                  20: (Prepare.compare,), 21: (Prepare.equal_before,), 22: (Prepare.join_ranks,),
                  23: (Prepare.sum_ranks,), 24: (Prepare.choose, Prepare.pick), 25: (Prepare.sum_picked,),
                  26: (Prepare.invert,), 27: (Prepare.gates, Prepare.gates_upper), 28: (Prepare.gates_apart,)}

            def gate_y(c, e):
                dve.wait_ge(h_used, HSTEPS * c + FSL * (e + 1))
                dve.wait_ge(spread_ready, EXPERTS * c + (e + 1))
                if e >= 2:
                    dve.wait_ge(acc_done, ADDS * c + (1 + max(e - 2, 1)))
                nc.vector.scalar_tensor_tensor(out=gated[:, e % 2, :], in0=ps_y[e % 2][:], scalar=b2[:, e:e + 1],
                                               in1=gate_all[:, e % 2, :], op0=ALU.add,
                                               op1=ALU.mult).then_inc(gated_ready, 1)

            def add_rows(slot):
                rows = rows_at(slot)
                nc.vector.tensor_tensor(rows, rows, ps_t[:].rearrange("p (t d) -> p t d", t=TPC),
                                        ALU.add).then_inc(x_updated, 1)

            def split_weights(e):
                dve.wait_ge(w1_upper, e + 1)
                nc.vector.tensor_copy(w2_hi[:, e, :], w2_raw[:, e % RAW, :]).then_inc(w2_upper, 1)
                nc.vector.tensor_tensor(w1_lo[:, e, :], w1_raw[:, e % RAW, :], w1_hi[:, e, :].bitcast(F32),
                                        ALU.subtract).then_inc(w1_lower, 1)

            def split_hidden(c, n):
                dve.wait_ge(relu_done, HSTEPS * c + (n + 1))
                nc.vector.tensor_copy(h_hi[:, n % SLOTS, :], h[:, n % SLOTS, :]).then_inc(hhi_ready, 1)
                if n % 2:
                    even = (n - 1) % SLOTS
                    dve.wait_ge(hhi_ready, HSTEPS * c + n)
                    nc.vector.tensor_tensor(h_lo[:, even, :], h[:, even, :], h_hi[:, even, :].bitcast(F32),
                                            ALU.subtract).then_inc(hlo_even, 1)

            if load_x is not None:
                dve.wait_ge(first_in, 16)
            chunk = Prepare(0, 0)
            for n in sorted(AT):
                for stage in AT[n]:
                    if stage is Prepare.lower:
                        dve.wait_ge(wr_upper, 1)
                        nc.vector.tensor_tensor(wr_parts[:, EXPERTS:], wr_raw[:], wr_parts[:, 0:EXPERTS].bitcast(F32),
                                                ALU.subtract).then_inc(wr_lower, 1)
                        split_weights(0)
                    if stage is Prepare.compare:
                        dve.wait_ge(consts, 8)
                    stage(chunk)
            nc.vector.memset(x_rows[:, 0:TPC, :], 0.0).then_inc(gated_ready, 1)
            nc.vector.memset(x_rows[:, (CHUNKS + 1) * TPC:, :], 0.0).then_inc(gated_ready, 1)
            for n in range(LAG):
                split_hidden(0, n)
            for e in range(1, EXPERTS):
                split_weights(e)
            if load_x is not None:
                dve.wait_ge(rows_in, 16 * (CHUNKS - 1))

            with dve.Fori(0, CHUNKS // 2) as pair:
                for half in range(2):
                    c = 2 * pair + half
                    following = Prepare(c + 1, 1 - half)
                    for n in range(HSTEPS):
                        split_hidden(c, n + LAG)
                        for stage in AT.get(n, ()):
                            stage(following)
                        if n == 6:
                            dve.wait_ge(outT_done, c + 1)
                            add_rows(c)
                        if n % FSL == FSL - 1:
                            gate_y(c, n // FSL)
            dve.wait_ge(outT_done, CHUNKS + 1)
            add_rows(CHUNKS)

        @block.tensor
        def _(pe):
            def transpose_rows(k):
                pe.wait_ge(xn_ready, k + 1)
                for t in range(TPC):
                    last = nc.tensor.transpose(ps_t[:, t * P:(t + 1) * P], xn[:, t, :], ident[:])
                last.then_inc(xT_done, 1)

            def logits_of(k, slot):
                pe.wait_ge(xlo_ready, k + 1)
                for t in range(TPC):
                    out = ps_t[:, t * 2 * EXPERTS:(t + 1) * 2 * EXPERTS]
                    cols = slice(t * P, (t + 1) * P)
                    nc.tensor.matmul(out, xT_hi[:, slot, cols], wr_parts[:], start=True, stop=False)
                    last = nc.tensor.matmul(out, xT_lo[:, slot, cols], wr_parts[:], start=False, stop=True)
                last.then_inc(logits_done, 1)

            def transpose_gates(k):
                pe.wait_ge(gate_ready, k + 1)
                for t in range(TPC):
                    last = nc.tensor.transpose(ps_t[0:2 * EXPERTS, t * P:(t + 1) * P], gate_parts[:, t, :], ident[:])
                last.then_inc(gateT_done, 1)

            def transpose_sum(done):
                pe.wait_ge(acc_done, done)
                for t in range(TPC):
                    last = nc.tensor.transpose(ps_t[:, t * P:(t + 1) * P], acc[:, t * P:(t + 1) * P], ident[:])
                last.then_inc(outT_done, 1)

            def hidden(c, n, slot):
                e, f = divmod(n % HSTEPS, FSL)
                if f == 0:
                    pe.wait_ge(w1_lower, e + 1)
                if n >= 4:
                    pe.wait_ge(relu_done, HSTEPS * c + (n - 3))
                fs, out = slice(f * P, (f + 1) * P), ps_h[n % 4][:]
                nc.tensor.matmul(out, w1_hi[:, e, fs], xT_hi[:, slot, :], start=True, stop=False)
                nc.tensor.matmul(out, w1_hi[:, e, fs], xT_lo[:, slot, :], start=False, stop=False)
                nc.tensor.matmul(out, w1_lo[:, e, fs], xT_hi[:, slot, :], start=False, stop=True).then_inc(h_done, 1)

            def second(c, n):
                e, f = divmod(n, FSL)
                if f == 0:
                    pe.wait_ge(gated_ready, EXPERTS * c + (e + 1))
                    pe.wait_ge(w2_lower, e + 1)
                wait_hlo(pe, c, n)
                fs, out = slice(f * P, (f + 1) * P), ps_y[e % 2][:]
                nc.tensor.matmul(out, w2_hi[:, e, fs], h_hi[:, n % SLOTS, :], start=(f == 0), stop=False)
                nc.tensor.matmul(out, w2_hi[:, e, fs], h_lo[:, n % SLOTS, :], start=False, stop=False)
                nc.tensor.matmul(out, w2_lo[:, e, fs], h_hi[:, n % SLOTS, :], start=False,
                                 stop=(f == FSL - 1)).then_inc(h_used, 1)

            pe.wait_ge(consts, 8)
            transpose_rows(0)
            pe.wait_ge(wr_lower, 1)
            logits_of(0, 0)
            for n in range(LAG):
                hidden(0, n, 0)
            transpose_gates(0)
            pe.wait_ge(spread_set, 1)
            with pe.Fori(0, CHUNKS // 2) as pair:
                for half in range(2):
                    c = 2 * pair + half
                    for n in range(HSTEPS):
                        e, f = divmod(n, FSL)
                        if f == 0:
                            if e == 0:
                                pe.wait_ge(gateT_ready, c + 1)
                            else:
                                pe.wait_ge(spread_ready, EXPERTS * c + e)
                            nc.tensor.matmul(ps_g[:], spread_r[:, e, :], gateT[:, half, :], start=True,
                                             stop=True).then_inc(spread_done, 1)
                        hidden(c, n + LAG, half if n + LAG < HSTEPS else 1 - half)
                        if n == 4:
                            transpose_sum(ADDS * c + 1)
                        if n == 9:
                            pe.wait_ge(x_updated, c + 1)
                            transpose_rows(c + 1)
                        if n == 15:
                            logits_of(c + 1, 1 - half)
                        if n == 29:
                            transpose_gates(c + 1)
                        second(c, n)
            transpose_sum(ADDS * CHUNKS + 1)

class Item:

    def __init__(self, kind, slot, before, head=0, tile=0):
        self.kind, self.slot, self.head, self.tile = kind, slot, head, tile
        self.done = before[0] + 1
        self.hi = before[1] + {"xT": 1, "K": 1, "Q": 2}.get(kind, 0)
        self.act = before[2] + (kind in ("V", "maxT"))
        self.dve = before[3] + (kind in ("xT", "K", "Q", "peak", "out"))
        self.last_is_act = self.act > before[2]

def plan_items(groups):
    count, total, placed = (0, 0, 0, 0), 0, {}
    flat = []
    for place, kinds in groups:
        for kind, head, tile in kinds:
            item = Item(kind, total % 2, count, head, tile)
            count = (item.done, item.hi, item.act, item.dve)
            total += 1
            item.two_before = flat[-2] if len(flat) >= 2 else None
            flat.append(item)
            placed.setdefault(place, []).append(item)
    return placed, count

def attention_phase(nc, x_rows, wq_in, wk_in, wv_in, wo_in, inv_dram):
    with ExitStack() as ctx:
        def sb(name, shape, dt=F32):
            return ctx.enter_context(nc.sbuf_tensor(name, shape, dt))

        def psum(name, width=CHUNK):
            return ctx.enter_context(nc.psum_tensor(name, [P, width], F32))

        def sem(name):
            return ctx.enter_context(nc.semaphore(name))

        SCALE = float(HEAD) ** -0.5
        FRONT = ST = SEQ // P
        VT = TPC
        QC = SEQ // CHUNK
        PAIRS = HEADS // 2
        LAG = 4
        RING = LAG + 1

        wq_hi = sb("wq_hi", [P, HEADS * HEAD], F32R)
        wq_lo = sb("wq_lo", [P, HEADS * HEAD], F32R)
        wk_hi = sb("wk_hi", [P, KV_HEADS, 2, HEAD], F32R)
        wk_lo = sb("wk_lo", [P, KV_HEADS, 2, HEAD], F32R)
        wv_hi = sb("wv_hi", [P, KV_HEADS * HEAD], F32R)
        wv_lo = sb("wv_lo", [P, KV_HEADS * HEAD], F32R)
        wo = sb("wo", [P, PAIRS, P])
        ident = sb("ident_a", [P, P])
        ident_b = sb("ident_b", [P, P], BF16)
        mask_q = sb("mask_q", [P, SEQ], BF16)
        mask_k = sb("mask_k", [P, P], BF16)
        minus_half = sb("minus_half_a", [P, ST])
        row_sum = sb("row_sum_a", [P, ST])
        mean = sb("mean_a", [P, ST])
        sq_sum = sb("sq_sum_a", [P, ST])
        var_eps = sb("var_eps_a", [P, ST])
        rstd = sb("rstd_a", [P, ST])
        xT_hi = sb("xT_hi_a", [P, SEQ], F32R)
        xT_lo = sb("xT_lo_a", [P, SEQ], F32R)
        q_both = [sb(f"q_both{i}", [P, QPK, SEQ], F32R) for i in range(2)]
        q_max = [sb(f"q_max{i}", [P, QPK, SEQ], F32R) for i in range(2)]
        k_twice = [sb(f"k_twice{i}", [P, SEQ], F32R) for i in range(2)]
        k_low = [sb(f"k_low{i}", [P, SEQ], F32R) for i in range(2)]
        v_raw = sb("v_raw", [P, ST, KV_HEADS * HEAD])
        v_hi = [sb(f"v_hi{i}", [P, ST, HEAD + 2], F32R) for i in range(2)]
        v_lo = [sb(f"v_lo{i}", [P, ST, HEAD], F32R) for i in range(2)]
        peak_there = sb("peak_there", [P, 2, QPK * ST], BF16)
        neg_max = sb("neg_max", [P, 2, QPK * ST])
        max_rows = sb("max_rows", [QPK * ST, 2, P], F32R)
        probs = sb("probs", [P, LAG, CHUNK])
        probs_hi = sb("probs_hi", [P, RING, CHUNK], F32R)
        probs_lo = sb("probs_lo", [P, RING, CHUNK], F32R)
        sums = sb("sums", [1, SEQ])
        sums_t = sb("sums_t", [P, 2, ST])
        inv_t = sb("inv_t", [P, 2, ST])
        inv_all = sb("inv_all", [P, 2, SEQ])
        oT = sb("oT", [P, 4, SEQ])
        wq_raw = oT[:, 0, :]
        wk_raw = oT[:, 1, 0:KV_HEADS * 2 * HEAD].rearrange("d (g c e) -> d g c e", g=KV_HEADS, c=2)
        wv_raw = oT[:, 2, 0:KV_HEADS * HEAD]
        squares = v_raw[:, :, 0:P]
        centred = v_raw[:, :, P:2 * P]

        ps_s = [psum("ps_s0"), psum("ps_s1")]
        ps_v = [psum("ps_v0"), psum("ps_v1")]
        ps_i = [psum("ps_i0", 2 * CHUNK), psum("ps_i1", 2 * CHUNK)]

        w_in = sem("w_in_a")
        consts = sem("consts_a")
        filled = sem("filled")
        FILLS = 7
        w_upper = sem("w_upper_a")
        w_lower = sem("w_lower_a")
        prep = sem("prep_a")
        var_ready = sem("var_ready_a")
        rstd_ready = sem("rstd_ready_a")
        xn_ready = sem("xn_ready_a")
        item_done = sem("item_done")
        hi_ready = sem("hi_ready")
        act_read = sem("act_read")
        dve_read = sem("dve_read")
        max_in = sem("max_in")
        v_upper = sem("v_upper")
        v_lower = sem("v_lower")
        lo_done = sem("lo_done")
        q_twice = sem("q_twice")
        s_done = sem("s_done")
        exp_done = sem("exp_done")
        pv_done = sem("pv_done")
        copied = sem("copied")
        sums_out = sem("sums_out")
        sums_in = sem("sums_in")
        inverted = sem("inverted")
        inv_out = sem("inv_out")
        inv_in = [sem("inv_in_even"), sem("inv_in_odd")]
        scaled = sem("scaled")

        ORDER = [[0, 3, 1, 2], [0, 5, 1, 6, 2, 7, 3, 4]]
        STEPS = [(j, qc, kt) for j in range(QPK) for qc in range(QC) for kt in ORDER[qc]]
        NS = len(STEPS)
        NB = KV_HEADS * NS
        CHUNKS_U = QPK * QC

        def cols_of(qc, kt):
            first = max(qc * CHUNK, kt * P)
            return first, first - qc * CHUNK

        PEAKS_AT = ((0, 7), (2,), (1,), (6,), (3,), (5,), (4,))
        Q_READ = 4

        def unit_groups(g, first, tail=()):
            late = 3 if first else 1
            groups = [(0, [("xT", 0, 0)]), (1, [("xT", 0, 1)]), (late + 1, [("V", 0, 0)]),
                      (late + 2, [("V", 0, 1)])] if first else []
            place = late + 3 + Q_READ
            groups += [(late, [("K", 0, 0)]), (late + 3, [("Q", 0, 0)])]
            for j in range(QPK):
                if j == 1:
                    groups += [(place, [("Q", 2, 0)])]
                    place += Q_READ
                for tiles in PEAKS_AT:
                    place += 1
                    groups += [(place, [("peak", j, t) for t in tiles])]
            groups += [(place + 4, [("maxT", 0, 0)])] + list(tail)
            assert place + 4 < NS
            groups.sort(key=lambda group: (group[0], group[1][0][0] == "Q"))
            return [((g, step), kinds) for step, kinds in groups]

        NORM_STAGES = 7
        NORM = (KV_HEADS - 1) * NS - 10
        RSTD = NORM + 6
        BOTH = 2
        OUT = 30
        SPLIT = 9

        BODY, PER = plan_items([x for g in range(KV_HEADS) for x in unit_groups(
                                    g, g == KV_HEADS - 1, [(OUT, [("out", g, BOTH)])] if g < KV_HEADS - 1 else [])]
                               + [((KV_HEADS, 0), [("out", KV_HEADS - 1, BOTH)])])
        FIRST, PRE = plan_items(unit_groups(0, True))
        FIRST_ITEMS = [item for place in sorted(FIRST) for item in FIRST[place]]
        for plan in (FIRST, BODY):
            for (g, step), items in plan.items():
                for item in items:
                    if item.kind == "peak":
                        item.queries = next(q for (unit, _), group in plan.items() for q in group
                                            if unit == g and q.kind == "Q" and q.head == item.head // 2 * 2)
        FIRST_V, BODY_V = [max(item.act for items in plan.values() for item in items if item.kind == "V")
                           for plan in (FIRST, BODY)]
        SECOND = {(g, s + 1): [item for item in items if item.kind == "Q"] for (g, s), items in BODY.items()}
        LAST = plan_items([(0, [("out", 0, 0), ("out", 0, 1)])])[0][0]
        assert PER[0] % 2 == 0 and PRE[0] % 2 == 0

        def base(b, which):
            return 0 if b is None else PRE[which] + PER[which] * b

        def unit_after(g):
            nxt = (g + 1) % KV_HEADS
            return nxt, nxt % 2

        def steps_through(g, j, qc):
            return g * NS + STEPS.index((j, qc, ORDER[qc][-1])) + 1

        ENDED = {steps_through(g, j, qc) + LAG: (g, j, qc) for g in range(KV_HEADS) for j in range(QPK)
                 for qc in range(QC)}

        block = ctx.enter_context(nc.Block())

        @block.sync
        def _(sp):
            sp.dma_start(wk_raw, wk_in.rearrange("d (g c e) -> d g c e", g=KV_HEADS, c=2)).then_inc(w_in, 16)
            sp.dma_start(wv_raw, wv_in).then_inc(w_in, 16)
            sp.dma_start(wq_raw, wq_in).then_inc(w_in, 16)
            sp.dma_start(wo[:], wo_in.rearrange("(n p) d -> p n d", p=P)).then_inc(w_in, 16)

            def turn_sums(b, head):
                slot, pair, side = head % 2, head // 2, (head % 2) * HEAD
                n = HEADS * b + (head + 2)
                sp.wait_ge(sums_out, QC * n + QC)
                sp.dma_start(sums_t[:, slot, :], sums[:].rearrange("o (p t) -> o p t", t=ST)).then_inc(sums_in, 16)
                sp.wait_ge(inverted, n + 1)
                sp.dma_start(inv_dram[slot].rearrange("(p t) -> p t", t=ST), inv_t[:, slot, :]).then_inc(inv_out, 16)
                sp.wait_ge(inv_out, 16 * n + 16)
                sp.dma_start(inv_all[side:side + HEAD, pair % 2, :],
                             inv_dram[slot:slot + 1, :].to_broadcast([HEAD, SEQ])).then_inc(inv_in[slot], 16)

            turn_sums(0, -2)
            turn_sums(0, -1)
            with sp.Fori(0, BATCH) as b:
                for head in range(HEADS):
                    turn_sums(b, head)

        @block.gpsimd
        def _(pool):
            nc.gpsimd.memset(ident[:], 0.0).then_inc(consts, 1)
            nc.gpsimd.memset(ident_b[:], 0.0).then_inc(consts, 1)
            nc.gpsimd.memset(mask_q[:], 0.0).then_inc(consts, 1)
            nc.gpsimd.memset(mask_k[:], 0.0).then_inc(consts, 1)
            nc.gpsimd.memset(minus_half[:], -0.5).then_inc(consts, 1)
            pool.wait_ge(consts, 5)
            for m in (ident, ident_b):
                nc.gpsimd.affine_select(out=m[:], in_=m[:], compare_op=ALU.not_equal, fill=1.0, base=0,
                                        pattern=[[-1, P]], channel_multiplier=1).then_inc(consts, 1)
            nc.gpsimd.affine_select(out=mask_q[:, SEQ - P:], in_=mask_q[:, SEQ - P:], compare_op=ALU.is_ge,
                                    fill=STRUCK, base=0, pattern=[[-1, P]], channel_multiplier=1).then_inc(consts, 1)
            nc.gpsimd.affine_select(out=mask_k[:], in_=mask_k[:], compare_op=ALU.is_ge, fill=STRUCK, base=0,
                                    pattern=[[1, P]], channel_multiplier=-1).then_inc(consts, 1)

            def rstd_of(batch):
                pool.wait_ge(var_ready, batch + 1)
                nc.gpsimd.tensor_tensor(rstd[:], var_eps[:], minus_half[:], ALU.pow).then_inc(rstd_ready, 1)

            rstd_of(0)
            pool.wait_ge(rstd_ready, 1)
            for slot in range(2):
                nc.gpsimd.memset(k_low[slot][HEAD:HEAD + 1, :].bitcast(F32), 1.0).then_inc(filled, 1)
                pool.wait_ge(filled, 2 * slot + 1)
                nc.gpsimd.memset(v_hi[slot][:, :, HEAD:].bitcast(F32), 1.0).then_inc(filled, 1)
                pool.wait_ge(filled, 2 * slot + 2)
            nc.gpsimd.memset(x_rows[:, 0:FRONT, :], 0.0).then_inc(filled, 1)
            nc.gpsimd.memset(x_rows[:, FRONT + BATCH * ST:, :], 0.0).then_inc(filled, 1)
            pool.wait_ge(w_lower, 1)
            nc.gpsimd.memset(oT[:, 2:4, :], 0.0).then_inc(filled, 1)
            pool.wait_ge(filled, FILLS)
            nc.gpsimd.memset(sums[:], 1.0).then_inc(sums_out, 2 * QC)
            with pool.Fori(0, BATCH) as b:
                for n in range(NB):
                    if n == RSTD:
                        rstd_of(b + 1)
                    width = CHUNK - cols_of(*STEPS[n % NS][1:])[1]
                    pool.wait_ge(exp_done, NB * b + (n + 1))
                    nc.gpsimd.tensor_tensor(probs_lo[:, n % RING, 0:width], probs[:, n % LAG, 0:width],
                                            probs_hi[:, n % RING, 0:width].bitcast(F32),
                                            ALU.subtract).then_inc(lo_done, 1)

        @block.scalar
        def _(act):
            def read(item, b, slot, g):
                src = ps_i[item.slot]
                if item.kind in ("peak", "out"):
                    return
                act.wait_ge(item_done, base(b, 0) + item.done)
                if item.kind == "xT":
                    half = slice(item.tile * CHUNK, (item.tile + 1) * CHUNK)
                    nc.scalar.activation(xT_hi[:, half], src[:, 0:CHUNK], ACT.Copy).then_inc(hi_ready, 1)
                elif item.kind == "K":
                    nc.scalar.activation(k_twice[slot][:], src[:], ACT.Copy).then_inc(hi_ready, 1)
                elif item.kind == "V":
                    nc.scalar.activation(v_raw[:, item.tile * VT:(item.tile + 1) * VT, :],
                                         src[:].rearrange("p (t d) -> p t d", t=VT), ACT.Copy).then_inc(act_read, 1)
                elif item.kind == "Q":
                    nc.scalar.activation(q_both[slot][0:HEAD, item.head, :], src[0:HEAD, :],
                                         ACT.Copy).then_inc(hi_ready, 1)
                elif item.kind == "maxT":
                    nc.scalar.activation(max_rows[:, slot, :], src[0:QPK * ST, 0:P], ACT.Copy).then_inc(act_read, 1)
                    act.wait_ge(act_read, base(b, 2) + item.act)
                    row = q_max[slot][HEAD:HEAD + 1, :, :].bitcast(F32)
                    act.dma_start(row.rearrange("o j (t s) -> o (j t) s", s=P),
                                  max_rows[:, slot, :].bitcast(F32)).then_inc(max_in, 16)

            def read_second(item, slot):
                nc.scalar.activation(q_both[slot][0:HEAD, item.head + 1, :], ps_i[item.slot][HEAD:2 * HEAD, :],
                                     ACT.Copy).then_inc(hi_ready, 1)

            def upper_values(b, g, slot):
                act.wait_ge(act_read, base(b, 2) + (FIRST_V if b is None else BODY_V if g == 0 else 0))
                nc.scalar.activation(v_hi[slot][:, :, 0:HEAD], v_raw[:, :, g * HEAD:(g + 1) * HEAD],
                                     ACT.Copy).then_inc(v_upper, 1)

            def take_sums(b, g, j, qc):
                head, chunk = g * QPK + j, g * CHUNKS_U + j * QC + qc
                act.wait_ge(pv_done, NB * b + steps_through(g, j, qc))
                if qc == 0:
                    act.wait_ge(sums_in, 16 * HEADS * b + 16 * (head + 2))
                nc.scalar.activation(sums[0:1, qc * CHUNK:(qc + 1) * CHUNK],
                                     ps_v[chunk % 2][HEAD:HEAD + 1, :], ACT.Copy).then_inc(sums_out, 1)

            act.wait_ge(w_in, 64)
            nc.scalar.activation(wk_hi[:], wk_raw, ACT.Copy)
            nc.scalar.activation(wv_hi[:], wv_raw, ACT.Copy)
            nc.scalar.activation(wq_hi[:], wq_raw, ACT.Copy).then_inc(w_upper, 1)
            for item in FIRST_ITEMS:
                read(item, None, 0, 0)
                if item.kind == "Q":
                    read_second(item, 0)
            upper_values(None, 0, 0)
            with act.Fori(0, BATCH) as b:
                for n in range(NB):
                    g, s = n // NS, n % NS
                    width = CHUNK - cols_of(*STEPS[s][1:])[1]
                    act.wait_ge(s_done, NB * b + (n + 1))
                    if n >= LAG:
                        act.wait_ge(lo_done, NB * b + (n - LAG + 1))
                    nc.scalar.activation(probs[:, n % LAG, 0:width], ps_s[n % 2][:, 0:width], ACT.Exp, scale=SCALE)
                    nc.scalar.activation(probs_hi[:, n % RING, 0:width], ps_s[n % 2][:, 0:width], ACT.Exp,
                                         scale=SCALE).then_inc(exp_done, 1)
                    for item in SECOND.get((g, s), []):
                        read_second(item, unit_after(g)[1])
                    for item in BODY.get((g, s), []):
                        read(item, b, unit_after(g)[1], g)
                    if s == SPLIT:
                        upper_values(b, *unit_after(g))
                    if n in ENDED:
                        take_sums(b, *ENDED[n])
                take_sums(b, KV_HEADS - 1, QPK - 1, QC - 1)
                for item in BODY[(KV_HEADS, 0)]:
                    read(item, b, 0, 0)
            act.wait_ge(max_in, 16 * (KV_HEADS * BATCH + 1))

        @block.vector
        def _(dve):
            def norm(batch, stage):
                if isinstance(batch, int):
                    rows = x_rows[:, FRONT + batch * ST:FRONT + (batch + 1) * ST, :]
                else:
                    rows = x_rows[:, bass.ds(batch * ST + FRONT, ST), :]

                def over(stat):
                    return stat[:].unsqueeze(2).to_broadcast([P, ST, P])

                if stage == 0:
                    nc.vector.tensor_reduce(row_sum[:], rows, AX.X, ALU.add).then_inc(prep, 1)
                    return
                if stage < NORM_STAGES - 1:
                    dve.wait_ge(prep, 5 * batch + stage)
                if stage == 1:
                    nc.vector.tensor_scalar(mean[:], row_sum[:], 1.0 / P, None, ALU.mult).then_inc(prep, 1)
                elif stage == 2:
                    nc.vector.tensor_tensor(centred, rows, over(mean), ALU.subtract).then_inc(prep, 1)
                elif stage == 3:
                    nc.vector.tensor_tensor(squares, centred, centred, ALU.mult).then_inc(prep, 1)
                elif stage == 4:
                    nc.vector.tensor_reduce(sq_sum[:], squares, AX.X, ALU.add).then_inc(prep, 1)
                elif stage == 5:
                    nc.vector.tensor_scalar(var_eps[:], sq_sum[:], 1.0 / P, EPS, ALU.mult,
                                            ALU.add).then_inc(var_ready, 1)
                else:
                    dve.wait_ge(rstd_ready, batch + 1)
                    nc.vector.tensor_tensor(centred, centred, over(rstd), ALU.mult).then_inc(xn_ready, 1)

            def lower(out, item, b, src, hi):
                dve.wait_ge(hi_ready, base(b, 1) + item.hi)
                return nc.vector.tensor_tensor(out, src, hi.bitcast(F32), ALU.subtract)

            def read(item, b, slot, g):
                src = ps_i[item.slot]
                if item.kind == "xT":
                    half = slice(item.tile * CHUNK, (item.tile + 1) * CHUNK)
                    lower(xT_lo[:, half], item, b, src[:, 0:CHUNK], xT_hi[:, half]).then_inc(dve_read, 1)
                elif item.kind == "K":
                    lower(k_low[slot][0:HEAD, :], item, b, src[0:HEAD, :],
                          k_twice[slot][0:HEAD, :]).then_inc(dve_read, 1)
                elif item.kind == "Q":
                    read_head(item, b, slot, 0)
                elif item.kind == "peak":
                    dve.wait_ge(item_done, base(b, 0) + item.done)
                    at = item.head * ST + item.tile
                    width = (item.tile + 1) * P
                    nc.vector.tensor_copy(peak_there[:, slot, at:at + 1], minus_half[:, 0:1])
                    nc.vector.tensor_tensor_reduce(src[:, 0:width], src[:, 0:width], mask_q[:, SEQ - width:], -1.0,
                                                   -STRUCK, ALU.add, ALU.min,
                                                   neg_max[:, slot, at:at + 1]).then_inc(dve_read, 1)
                elif item.kind == "out":
                    dve.wait_ge(item_done, base(b, 0) + item.done)
                    shift = 0 if item.head == 0 else ST
                    rows = x_rows[:, bass.ds(b * ST + shift, ST), :] if not isinstance(b, int) else \
                        x_rows[:, b * ST + shift:(b + 1) * ST + shift, :]
                    nc.vector.tensor_tensor(rows, rows, src[:].rearrange("p (t d) -> p t d", t=ST),
                                            ALU.add).then_inc(dve_read, 1)

            def read_head(item, b, slot, n):
                upper = q_both[slot][0:HEAD, item.head + n, :]
                dve.wait_ge(hi_ready, base(b, 1) + item.hi - 1 + n)
                last = nc.vector.tensor_tensor(q_both[slot][HEAD:2 * HEAD, item.head + n, :],
                                               ps_i[item.slot][n * HEAD:(n + 1) * HEAD, :], upper.bitcast(F32),
                                               ALU.subtract)
                if n == 1:
                    last.then_inc(dve_read, 1)
                    both = slice(item.head, item.head + 2)
                    nc.vector.tensor_copy(q_max[slot][0:HEAD, both, :],
                                          q_both[slot][0:HEAD, both, :]).then_inc(q_twice, 1)

            def lower_values(b, g, slot):
                dve.wait_ge(v_upper, 1 if b is None else KV_HEADS * b + ((g - 1) % KV_HEADS + 2))
                nc.vector.tensor_tensor(v_lo[slot][:], v_raw[:, :, g * HEAD:(g + 1) * HEAD],
                                        v_hi[slot][:, :, 0:HEAD].bitcast(F32), ALU.subtract).then_inc(v_lower, 1)

            def take_values(b, g, j, qc):
                head, chunk = g * QPK + j, g * CHUNKS_U + j * QC + qc
                dve.wait_ge(pv_done, NB * b + steps_through(g, j, qc))
                side = slice((head % 2) * HEAD, (head % 2 + 1) * HEAD)
                nc.vector.tensor_copy(oT[side, head // 2 % 4, qc * CHUNK:(qc + 1) * CHUNK],
                                      ps_v[chunk % 2][0:HEAD, :]).then_inc(copied, 1)

            def invert_sums(b, head):
                dve.wait_ge(sums_in, 16 * HEADS * b + 16 * (head + 3))
                nc.vector.reciprocal(inv_t[:, head % 2, :], sums_t[:, head % 2, :]).then_inc(inverted, 1)

            def scale_pair(b, pair):
                for side in range(2):
                    dve.wait_ge(inv_in[side], 16 * PAIRS * b + 16 * (pair + 2))
                dve.wait_ge(copied, 2 + KV_HEADS * CHUNKS_U * b + QC * (2 * pair + 2))
                nc.vector.tensor_tensor(oT[:, pair % 4, :], oT[:, pair % 4, :], inv_all[:, pair % 2, :],
                                        ALU.mult).then_inc(scaled, 1)

            for stage in range(NORM_STAGES):
                norm(0, stage)
            dve.wait_ge(w_upper, 1)
            nc.vector.tensor_tensor(wk_lo[:], wk_raw, wk_hi[:].bitcast(F32), ALU.subtract).then_inc(copied, 2)
            nc.vector.tensor_tensor(wv_lo[:], wv_raw, wv_hi[:].bitcast(F32), ALU.subtract)
            nc.vector.tensor_tensor(wq_lo[:], wq_raw, wq_hi[:].bitcast(F32), ALU.subtract).then_inc(w_lower, 1)
            for item in FIRST_ITEMS:
                read(item, None, 0, 0)
                if item.kind == "Q":
                    read_head(item, None, 0, 1)
            lower_values(None, 0, 0)
            dve.wait_ge(filled, FILLS)
            invert_sums(0, -2)
            with dve.Fori(0, BATCH) as b:
                for n in range(NB):
                    g, s = n // NS, n % NS
                    if NORM <= n < NORM + NORM_STAGES:
                        norm(b + 1, n - NORM)
                    for item in SECOND.get((g, s), []):
                        read_head(item, b, unit_after(g)[1], 1)
                    for item in BODY.get((g, s), []):
                        read(item, b, unit_after(g)[1], g)
                    if s == SPLIT:
                        lower_values(b, *unit_after(g))
                    if n in ENDED:
                        take_values(b, *ENDED[n])
                    if s % 12 == 9:
                        invert_sums(b, g * QPK + s // 12 - 1)
                    if s in (17, 41):
                        scale_pair(b, 2 * g + s // 24 - 1)
                take_values(b, KV_HEADS - 1, QPK - 1, QC - 1)
                for item in BODY[(KV_HEADS, 0)]:
                    read(item, b, 0, 0)
            invert_sums(BATCH - 1, HEADS - 1)
            scale_pair(BATCH - 1, PAIRS - 1)
            for item in LAST:
                dve.wait_ge(dve_read, base(BATCH, 3) + item.dve - 1)
                read(item, BATCH, 0, 0)

        @block.tensor
        def _(pe):
            def split_product(out, w_h, w_l, x_h, x_l):
                nc.tensor.matmul(out, w_h, x_h, start=True, stop=False)
                nc.tensor.matmul(out, w_h, x_l, start=False, stop=False)
                return nc.tensor.matmul(out, w_l, x_h, start=False, stop=True)

            def write(item, b, slot, g):
                if item.two_before is None:
                    if b is not None:
                        pe.wait_ge(act_read, base(b, 2))
                        pe.wait_ge(dve_read, base(b, 3))
                elif item.two_before.last_is_act:
                    pe.wait_ge(act_read, base(b, 2) + item.two_before.act)
                else:
                    pe.wait_ge(dve_read, base(b, 3) + item.two_before.dve)
                dst = ps_i[item.slot]
                halves = [slice(c * CHUNK, (c + 1) * CHUNK) for c in range(QC)]
                if item.kind == "xT":
                    pe.wait_ge(xn_ready, 1 if b is None else b + 2)
                    for t in range(TPC):
                        last = nc.tensor.transpose(dst[:, t * P:(t + 1) * P], centred[:, item.tile * TPC + t, :],
                                                   ident[:])
                elif item.kind == "K":
                    pe.wait_ge(dve_read, base(b, 3) + (item.dve - 1))
                    for c in halves:
                        last = split_product(dst[:, c], wk_hi[:, g, :, :].rearrange("p c e -> p (c e)"),
                                             wk_lo[:, g, :, :].rearrange("p c e -> p (c e)"), xT_hi[:, c], xT_lo[:, c])
                elif item.kind == "V":
                    for t in range(VT):
                        out = dst[:, t * KV_HEADS * HEAD:(t + 1) * KV_HEADS * HEAD]
                        ts = slice((item.tile * VT + t) * P, (item.tile * VT + t + 1) * P)
                        nc.tensor.matmul(out, xT_hi[:, ts], wv_hi[:], start=True, stop=False)
                        nc.tensor.matmul(out, xT_hi[:, ts], wv_lo[:], start=False, stop=False)
                        last = nc.tensor.matmul(out, xT_lo[:, ts], wv_hi[:], start=False, stop=True)
                elif item.kind == "Q":
                    hs = slice((g * QPK + item.head) * HEAD, (g * QPK + item.head + 2) * HEAD)
                    for c in halves:
                        last = split_product(dst[:, c], wq_hi[:, hs], wq_lo[:, hs], xT_hi[:, c], xT_lo[:, c])
                elif item.kind == "peak":
                    if item.head % 2 == 0 and item.tile == PEAKS_AT[0][0]:
                        pe.wait_ge(dve_read, base(b, 3) + item.queries.dve)
                    j, t = item.head, item.tile
                    query = q_both[slot][:, j, t * P:(t + 1) * P]
                    for c in range(t // TPC + 1):
                        end = min((c + 1) * CHUNK, (t + 1) * P)
                        last = nc.tensor.matmul(dst[:, c * CHUNK:end], query, k_twice[slot][:, c * CHUNK:end],
                                                start=True, stop=True)
                elif item.kind == "maxT":
                    pe.wait_ge(dve_read, base(b, 3) + item.dve)
                    last = nc.tensor.transpose(dst[0:QPK * ST, 0:P], neg_max[:, slot, :], ident[:])
                elif item.kind == "out":
                    chosen = (0, 1) if item.tile == BOTH else (item.tile,)
                    pe.wait_ge(scaled, PAIRS * b + 2 * item.head + chosen[-1])
                    for t in range(ST):
                        for p in chosen:
                            pair = (2 * item.head - 2 + p) % PAIRS
                            last = nc.tensor.matmul(dst[:, t * P:(t + 1) * P], oT[:, pair % 4, t * P:(t + 1) * P],
                                                    wo[:, pair, :], start=(p == chosen[0]), stop=(p == chosen[-1]))
                last.then_inc(item_done, 1)

            def scores(b, g, s):
                j, qc, kt = STEPS[s]
                slot = g % 2
                n = g * NS + s
                first, offset = cols_of(qc, kt)
                width = CHUNK - offset
                keys = slice(kt * P, (kt + 1) * P)
                queries = slice(first, first + width)
                if n >= 2:
                    pe.wait_ge(exp_done, NB * b + (n - 1))
                if s == 0:
                    pe.wait_ge(q_twice, QPK // 2 * KV_HEADS * b + QPK // 2 * (g + 1))
                    pe.wait_ge(max_in, 16 * KV_HEADS * b + 16 * (g + 1))
                out = ps_s[n % 2][:, 0:width]
                diagonal = first == kt * P
                nc.tensor.matmul(out, k_twice[slot][:, keys], q_both[slot][:, j, queries], start=True, stop=False)
                last = nc.tensor.matmul(out, k_low[slot][0:HEAD + 1, keys], q_max[slot][0:HEAD + 1, j, queries],
                                        start=False, stop=not diagonal)
                if diagonal:
                    last = nc.tensor.matmul(out[:, 0:P], ident_b[:], mask_k[:], start=False, stop=True)
                last.then_inc(s_done, 1)

            def values(b, g, s):
                j, qc, kt = STEPS[s]
                n = g * NS + s
                chunk = g * CHUNKS_U + j * QC + qc
                offset = cols_of(qc, kt)[1]
                if s == 0:
                    pe.wait_ge(v_lower, KV_HEADS * b + (g + 1))
                if kt == 0:
                    pe.wait_ge(copied, KV_HEADS * CHUNKS_U * b + (chunk + 1))
                    pe.wait_ge(sums_out, KV_HEADS * CHUNKS_U * b + (2 * QC - 1 + chunk))
                pe.wait_ge(exp_done, NB * b + (n + 1))
                upper, lower = probs_hi[:, n % RING, 0:CHUNK - offset], probs_lo[:, n % RING, 0:CHUNK - offset]
                nc.tensor.matmul(ps_v[chunk % 2][0:HEAD + 2, offset:], v_hi[g % 2][:, kt, :], upper,
                                 start=(kt == 0), stop=False)
                nc.tensor.matmul(ps_v[chunk % 2][0:HEAD, offset:], v_lo[g % 2][:, kt, :], upper, start=False,
                                 stop=False)
                pe.wait_ge(lo_done, NB * b + (n + 1))
                nc.tensor.matmul(ps_v[chunk % 2][0:HEAD + 2, offset:], v_hi[g % 2][:, kt, :], lower, start=False,
                                 stop=(kt == ORDER[qc][-1])).then_inc(pv_done, 1)

            pe.wait_ge(consts, 9)
            pe.wait_ge(w_lower, 1)
            for item in FIRST_ITEMS:
                write(item, None, 0, 0)
            pe.wait_ge(filled, FILLS)
            with pe.Fori(0, BATCH) as b:
                for n in range(NB):
                    g, s = n // NS, n % NS
                    scores(b, g, s)
                    for item in BODY.get((g, s), []):
                        write(item, b, unit_after(g)[1], unit_after(g)[0])
                    if n >= LAG:
                        values(b, (n - LAG) // NS, (n - LAG) % NS)
                for item in BODY[(KV_HEADS, 0)]:
                    write(item, b, 0, 0)
                for n in range(NB - LAG, NB):
                    values(b, n // NS, n % NS)
            for item in LAST:
                write(item, BATCH, 0, 0)

def macaron_kernel(nc, x_in, wq_in, wk_in, wv_in, wo_in, wr_in, w1_in, b1_in, w2_in, b2_in, x_out):
    rows_in = x_in.rearrange("(c t p) d -> c p t d", t=TPC, p=P)
    rows_out = x_out.rearrange("(c t p) d -> c p t d", t=TPC, p=P)
    with ExitStack() as ctx:
        rows_all = ctx.enter_context(nc.sbuf_tensor("rows_all", [P, IDLE + TOKENS // P + IDLE, P], F32))
        x_rows = rows_all[:, IDLE - TPC:, :]

        def load_x(sp, c, loaded):
            sp.dma_start(x_rows[:, (c + 1) * TPC:(c + 2) * TPC, :], rows_in[c]).then_inc(loaded, 16)

        def store_x(sp, c, stored):
            sp.dma_start(rows_out[bass.ds(c, 1)].rearrange("o p t d -> (o p) t d"),
                         x_rows[:, bass.ds((c + 1) * TPC, TPC), :]).then_inc(stored, 16)

        ffn_phase(nc, "f1", x_rows, w1_in, w2_in, b1_in, b2_in, wr_in, load_x=load_x)
        inv_dram = nc.dram_tensor("inv_dram", (2, SEQ), F32, kind="Internal").ap()
        attention_phase(nc, rows_all, wq_in, wk_in, wv_in, wo_in, inv_dram)
        ffn_phase(nc, "f2", x_rows, w1_in, w2_in, b1_in, b2_in, wr_in, store_x=store_x)

def kernel(L0_attn_hidden_states, L0_attn_Wq, L0_attn_Wk, L0_attn_Wv, L0_attn_Wo, L0_ffn_Wr, L0_ffn_W1, L0_ffn_b1,
           L0_ffn_W2, L0_ffn_b2):
    import concourse.bacc as bacc
    import numpy as np
    from concourse.bass_utils import run_bass_kernel_spmd

    keys = np.asarray(L0_attn_Wk).T.reshape(P, KV_HEADS, 1, HEAD)
    arrays = {
        "in_x": np.asarray(L0_attn_hidden_states).reshape(TOKENS, P),
        "in_wq": np.asarray(L0_attn_Wq).T,
        "in_wk": np.concatenate([keys, keys], axis=2).reshape(P, KV_HEADS * 2 * HEAD),
        "in_wv": np.asarray(L0_attn_Wv).T,
        "in_wo": np.asarray(L0_attn_Wo).T,
        "in_wr": np.asarray(L0_ffn_Wr),
        "in_w1": np.asarray(L0_ffn_W1),
        "in_b1": np.asarray(L0_ffn_b1).reshape(EXPERTS * FSL, P).T,
        "in_w2": np.asarray(L0_ffn_W2),
        "in_b2": np.asarray(L0_ffn_b2).T,
    }
    arrays = {name: np.ascontiguousarray(a) for name, a in arrays.items()}
    nc = bacc.Bacc("TRN2", target_bir_lowering=False, num_devices=1)
    aps = [nc.dram_tensor(name, a.shape, F32, kind="ExternalInput").ap() for name, a in arrays.items()]
    out = nc.dram_tensor("out_x", (TOKENS, P), F32, kind="ExternalOutput").ap()
    macaron_kernel(nc, *aps, out)
    result = run_bass_kernel_spmd(nc, [arrays], core_ids=[0]).results[0]["out_x"]
    return result.reshape(BATCH, SEQ, P)
```
